# Optimizing a Trainium2 kernel written in Bass

```python
import numpy as np
import jax
import jax.numpy as jnp

def _softmax(x, axis=-1):
    return jax.nn.softmax(x, axis=axis)

def _gelu(x):
    return jax.nn.gelu(x, approximate=True)

def _silu(x):
    return jax.nn.silu(x)

def _sigmoid(x):
    return jax.nn.sigmoid(x)

def _layernorm(x, axis=-1, eps=1e-05):
    m = jnp.mean(x, axis=axis, keepdims=True)
    v = jnp.var(x, axis=axis, keepdims=True)
    return (x - m) / jnp.sqrt(v + eps)

def _scatter_add(tgt, idx, src, axis=0):
    return tgt.at[idx].add(src)

def _segment_sum(src, seg, n):
    return jax.ops.segment_sum(src, seg, n)
kernel_name = 'mk_gnn_preln_d1_gnn_r32_b36566'

def setup_inputs(seed: int=0):
    np.random.seed(seed)
    _w = jnp.asarray

    def _rec_inputs():
        import jax
        import jax.numpy as jnp
        _gk = jax.random.key(seed)
        x = -0.000202 + 1 * jax.random.normal(jax.random.fold_in(_gk, 1), (50000, 128), jnp.float32)
        src = jax.random.randint(jax.random.fold_in(_gk, 2), (25000,), 0, 50000, jnp.int32)
        dst = jax.random.randint(jax.random.fold_in(_gk, 3), (25000,), 0, 50000, jnp.int32)
        _o = jnp.argsort(dst, stable=True)
        src = src[_o]
        dst = dst[_o]
        edge_attr_32 = 0.000279952 + 1.00013 * jax.random.normal(jax.random.fold_in(_gk, 11), (25000, 32), jnp.float32)
        node_vec = jax.random.uniform(jax.random.fold_in(_gk, 13), (50000,), jnp.float32, 0.0, 0.999884)
        return (x, src, dst, edge_attr_32, node_vec)
    x, src, dst, edge_attr_32, node_vec = _rec_inputs()

    def _L0_gnn_setup():
        import jax, jax.numpy as jnp
        import numpy as np
        N_NODES = 50000
        N_EDGES = 20000
        HIDDEN = 128
        EDGE_DIM = 32

        def _init_linear(key, fan_in, fan_out):
            kw, kb = jax.random.split(key)
            bound = 1.0 / np.sqrt(fan_in)
            W = jax.random.uniform(kw, (fan_in, fan_out), jnp.float32, -bound, bound)
            b = jax.random.uniform(kb, (fan_out,), jnp.float32, -bound, bound)
            return (W, b)

        def _layernorm(x, gamma, beta, eps=1e-05):
            mu = jnp.mean(x, axis=-1, keepdims=True)
            var = jnp.mean(jnp.square(x - mu), axis=-1, keepdims=True)
            return (x - mu) * jax.lax.rsqrt(var + eps) * gamma + beta
        key = jax.random.key(seed)
        ks = jax.random.split(key, 10)
        node_features = jax.random.normal(ks[0], (N_NODES, HIDDEN), jnp.float32)
        edge_index = jax.random.randint(ks[1], (2, N_EDGES), 0, N_NODES, jnp.int64)
        edge_features = jax.random.normal(ks[2], (N_EDGES, EDGE_DIM), jnp.float32)
        coordination = jax.random.uniform(ks[3], (N_NODES,), jnp.float32)
        msg_in = 2 * HIDDEN + EDGE_DIM + 2
        upd_in = 2 * HIDDEN + 1
        mW1, mb1 = _init_linear(ks[4], msg_in, HIDDEN)
        mW2, mb2 = _init_linear(ks[5], HIDDEN, HIDDEN)
        uW1, ub1 = _init_linear(ks[6], upd_in, HIDDEN)
        uW2, ub2 = _init_linear(ks[7], HIDDEN, HIDDEN)
        ln_gamma = jnp.ones((HIDDEN,), jnp.float32)
        ln_beta = jnp.zeros((HIDDEN,), jnp.float32)
        return {'node_features': node_features, 'edge_index': edge_index, 'edge_features': edge_features, 'coordination': coordination, 'mW1': mW1, 'mb1': mb1, 'mW2': mW2, 'mb2': mb2, 'uW1': uW1, 'ub1': ub1, 'uW2': uW2, 'ub2': ub2, 'ln_gamma': ln_gamma, 'ln_beta': ln_beta}
    _L0_gnn_all = _L0_gnn_setup()
    _L0_gnn_in = {k: v for k, v in _L0_gnn_all.items() if k in ('mW1', 'mb1', 'mW2', 'mb2', 'uW1', 'ub1', 'uW2', 'ub2', 'ln_gamma', 'ln_beta')}
    del _L0_gnn_all
    return {'x': x, 'src': src, 'dst': dst, 'edge_attr_32': edge_attr_32, 'node_vec': node_vec, 'L0_gnn_mW1': _L0_gnn_in['mW1'], 'L0_gnn_mb1': _L0_gnn_in['mb1'], 'L0_gnn_mW2': _L0_gnn_in['mW2'], 'L0_gnn_mb2': _L0_gnn_in['mb2'], 'L0_gnn_uW1': _L0_gnn_in['uW1'], 'L0_gnn_ub1': _L0_gnn_in['ub1'], 'L0_gnn_uW2': _L0_gnn_in['uW2'], 'L0_gnn_ub2': _L0_gnn_in['ub2'], 'L0_gnn_ln_gamma': _L0_gnn_in['ln_gamma'], 'L0_gnn_ln_beta': _L0_gnn_in['ln_beta']}

def reference(x, src, dst, edge_attr_32, node_vec, L0_gnn_mW1, L0_gnn_mb1, L0_gnn_mW2, L0_gnn_mb2, L0_gnn_uW1, L0_gnn_ub1, L0_gnn_uW2, L0_gnn_ub2, L0_gnn_ln_gamma, L0_gnn_ln_beta):
    import jax
    import jax.numpy as jnp

    def _L0_gnn_ref(node_features, edge_index, edge_features, coordination, mW1, mb1, mW2, mb2, uW1, ub1, uW2, ub2, ln_gamma, ln_beta):
        import jax, jax.numpy as jnp
        import numpy as np
        N_NODES = 50000
        N_EDGES = 20000
        HIDDEN = 128
        EDGE_DIM = 32

        def _init_linear(key, fan_in, fan_out):
            kw, kb = jax.random.split(key)
            bound = 1.0 / np.sqrt(fan_in)
            W = jax.random.uniform(kw, (fan_in, fan_out), jnp.float32, -bound, bound)
            b = jax.random.uniform(kb, (fan_out,), jnp.float32, -bound, bound)
            return (W, b)

        def _layernorm(x, gamma, beta, eps=1e-05):
            mu = jnp.mean(x, axis=-1, keepdims=True)
            var = jnp.mean(jnp.square(x - mu), axis=-1, keepdims=True)
            return (x - mu) * jax.lax.rsqrt(var + eps) * gamma + beta
        n_nodes = node_features.shape[0]
        src, dst = (edge_index[0], edge_index[1])
        edge_input = jnp.concatenate([node_features[src], node_features[dst], edge_features, coordination[src][:, None], coordination[dst][:, None]], axis=-1)
        h = jax.nn.silu(edge_input @ mW1 + mb1)
        messages = h @ mW2 + mb2
        aggregated = jax.ops.segment_sum(messages, dst, num_segments=n_nodes)
        update_input = jnp.concatenate([node_features, aggregated, coordination[:, None]], axis=-1)
        u = jax.nn.silu(update_input @ uW1 + ub1)
        upd = u @ uW2 + ub2
        return _layernorm(node_features + upd, ln_gamma, ln_beta)
    edge_index = jnp.stack([src, dst])
    h = jnp.maximum(_layernorm(x, axis=-1), 0.0)
    x = x + _L0_gnn_ref(h, edge_index, edge_attr_32, node_vec, L0_gnn_mW1, L0_gnn_mb1, L0_gnn_mW2, L0_gnn_mb2, L0_gnn_uW1, L0_gnn_ub1, L0_gnn_uW2, L0_gnn_ub2, L0_gnn_ln_gamma, L0_gnn_ln_beta)
    return x

_drawn_inputs = setup_inputs


def setup_inputs(seed=0):
    import zlib

    import numpy as np

    out = dict(_drawn_inputs(seed))
    spreads = {'L0_gnn_ln_gamma': (1.0, 0.2), 'L0_gnn_ln_beta': (0.0, 0.1)}
    factors = {'edge_attr_32': 8.0,
     'node_vec': 8.0,
     'L0_gnn_mW1': 5.093,
     'L0_gnn_mb1': 34.836,
     'L0_gnn_mW2': 4.941,
     'L0_gnn_mb2': 51.506,
     'L0_gnn_ub1': 6.929}
    for name, (base, spread) in spreads.items():
        noise = np.random.default_rng([zlib.crc32(name.encode()), seed]).standard_normal(out[name].shape)
        drawn = base * np.exp(spread * noise) if base else spread * noise
        out[name] = jnp.asarray(drawn.astype(out[name].dtype))
    for name, factor in factors.items():
        out[name] = (out[name] * factor).astype(out[name].dtype)
    return out
```

```python
from contextlib import ExitStack

import concourse.bass as bass
from concourse import mybir

P = 128
H = 128
EDGE_DIM = 32
NODES = 50000
EDGES = 25000
EPS = 1e-5

E_TILES = 4
E_STEP = E_TILES * P
EDGE_STEPS = -(-EDGES // E_STEP)
EDGES_PAD = EDGE_STEPS * E_STEP
N_TILES = 8
N_STEP = N_TILES * P
NODE_STEPS = -(-NODES // N_STEP)
NODES_PAD = NODE_STEPS * N_STEP
DUMMY = NODES_PAD
TABLE_ROWS = NODES_PAD + P

ROW = 1 + H
FEAT = 1 + EDGE_DIM + 1
SRC_ROW = 1 + EDGE_DIM + ROW

RING = 4
NEAR = 1024
SCATTER_LAG = 4
NODE_LAG = 6
ZERO_ROWS = 2048
ZERO_DMAS = NODES_PAD // ZERO_ROWS
N_PARTS = 9 * N_TILES
PART_GROUPS = 1 + -(-NODE_STEPS // N_TILES)
ZERO_FIRST = 8
MAGIC = 0x5F3759DF
NEWTON = 3

C_IDENT, C_LOWER, C_DUMMY, C_PLACE = 0, P, 2 * P, 2 * P + 1
EDGE_COLS = EDGES_PAD // P
C_COLS = C_PLACE + EDGE_COLS

WHOLE, EDGES_ONLY, NODES_ONLY = "whole", "edges", "nodes"


def wait(eng, semaphore, count):
    if isinstance(count, int) and count <= 0:
        return
    eng.wait_ge(semaphore, count)


def wait_apart(eng, semaphore, count, passed):
    if isinstance(count, int) and count <= 0:
        return
    eng.wait_ge(semaphore, count)
    eng.sem_inc(passed, 1)


class Step:

    def __init__(self, n, phase, quarter):
        self.n = n
        self.slot = phase % RING
        self.fills4 = quarter + phase // RING
        self.half = phase % 2
        self.fills2 = 2 * quarter + phase // 2


class Iteration:

    def __init__(self, mode, phase, quarter):
        self.mode = mode
        self.phase, self.quarter = phase, quarter
        self.n = RING * quarter + phase
        self.edges, self.nodes = mode != NODES_ONLY, mode != EDGES_ONLY
        self.lag = NODE_LAG if mode == WHOLE else 1

    def _step(self, shift, steps, present):
        n = self.n + shift
        if not present or (isinstance(n, int) and not 0 <= n < steps):
            return None
        return Step(n, self.phase + shift, self.quarter)

    def edge(self, shift):
        return self._step(shift, EDGE_STEPS, self.edges)

    def node(self, shift):
        return self._step(shift - self.lag, NODE_STEPS, self.nodes)

    def edges_upto(self, shift):
        if not self.edges:
            return EDGE_STEPS
        n = self.n + shift + 1
        return min(max(n, 0), EDGE_STEPS) if isinstance(n, int) else n

    def nodes_upto(self, shift):
        if not self.nodes:
            return 0
        n = self.n - self.lag + shift + 1
        return min(max(n, 0), NODE_STEPS) if isinstance(n, int) else n

    def stats_before(self):
        return self.n + (EDGE_STEPS if self.mode == NODES_ONLY else 0)


PIPELINES = {WHOLE: (NODE_LAG + 5, EDGE_STEPS - 2, NODE_STEPS + NODE_LAG + 3),
             EDGES_ONLY: (SCATTER_LAG + 4, EDGE_STEPS - 2, EDGE_STEPS + SCATTER_LAG),
             NODES_ONLY: (6, NODE_STEPS - 1, NODE_STEPS + 4)}


def run_pipeline(eng, mode, body):
    first, last, total = PIPELINES[mode]
    first = -(-first // RING)
    last = last // RING
    for n in range(first * RING):
        body(Iteration(mode, n % RING, n // RING))
    with eng.Fori(first, last) as quarter:
        for phase in range(RING):
            body(Iteration(mode, phase, quarter))
    for n in range(last * RING, total):
        body(Iteration(mode, n % RING, n // RING))


def gnn_layer(nc, rows, ends, dst_place, attr, node_vec, mW1, mb1, mW2, mb2, uW1, ub1, uW2, ub2,
              gamma, beta, consts, out):
    f32, bf16, i32 = mybir.dt.float32, mybir.dt.bfloat16, mybir.dt.int32
    ALU, ACT, AX = mybir.AluOpType, mybir.ActivationFunctionType, mybir.AxisListType

    ends_v = ends.rearrange("(s p t) c -> s p (t c)", p=P, t=E_TILES)
    dst_v = dst_place.rearrange("(s n) -> s n", n=E_STEP)
    attr_v = attr.rearrange("(s p t) f -> s p t f", p=P, t=E_TILES)
    rows_v = rows.rearrange("(s p j) f -> s p (j f)", p=P, j=N_TILES)
    out_v = out.rearrange("(s p j) f -> s p (j f)", p=P, j=N_TILES)
    table = nc.dram_tensor("table", (TABLE_ROWS, H), f32, kind="Internal").ap()
    table_v = table[0:NODES_PAD, :].rearrange("(s p j) f -> s p (j f)", p=P, j=N_TILES)

    ctx = ExitStack()
    with ctx:
        def sb(name, shape, dt=f32):
            return ctx.enter_context(nc.sbuf_tensor(name, shape, dt))

        def pb(name, shape, dt=f32):
            return ctx.enter_context(nc.psum_tensor(name, shape, dt))

        def sem(name):
            return ctx.enter_context(nc.semaphore(name))

        const = sb("const_sb", [P, C_COLS])
        ident, lower = const[:, C_IDENT:C_IDENT + P], const[:, C_LOWER:C_LOWER + P]
        dummy_row, place = const[:, C_DUMMY:C_DUMMY + 1], const[:, C_PLACE:C_PLACE + EDGE_COLS]
        ident_b = sb("ident_b", [P, P], bf16)
        w_src, w_dst, w_feat = sb("w_src", [P, H]), sb("w_dst", [P, H]), sb("w_feat", [FEAT, H])
        w_node, w_agg, w_msg, w_msg_t = sb("w_node", [P, H]), sb("w_agg", [P, H]), sb("w_msg", [P, H]), sb("w_msg_t", [P, H])
        w_fold, w_out = sb("w_fold", [P, H]), sb("w_out", [P, H])
        mb1_col, ub1_col, mb2_col, w_coord_col = (sb(n, [P, 1]) for n in ("mb1_col", "ub1_col", "mb2_col", "w_coord_col"))
        gamma_b, beta_b = sb("gamma_b", [P, 1, H]), sb("beta_b", [P, 1, H])
        bias_rest = sb("bias_rest", [1, 2, 3, H])
        bias_part = sb("bias_part", [1, 2, 3, H], bf16)
        bias_rows = sb("bias_rows", [96, 2, H], bf16)
        ones_rows = sb("ones_rows", [96, P], bf16)
        coord = sb("coord", [P, NODE_STEPS, N_TILES])
        coord_rest = sb("coord_rest", [P, NODE_STEPS, N_TILES])
        coord_part = sb("coord_part", [P, NODE_STEPS, N_TILES, 3, 3], bf16)
        wc_part = sb("wc_part", [P, 3], bf16)
        wc_rest = sb("wc_rest", [P, 3])
        wc_cols = sb("wc_cols", [P, N_TILES, N_TILES, 3, 3], bf16)
        wc_rows = sb("wc_rows", [N_PARTS, N_TILES, H], bf16)
        coord_t = sb("coord_t", [N_PARTS, NODE_STEPS, P], bf16)
        zeros = sb("zeros", [P, ZERO_ROWS])
        dst_all = sb("dst_all", [P, EDGE_COLS], i32)
        off_place, off_square = sb("off_place", [P, EDGE_COLS]), sb("off_square", [P, EDGE_COLS])
        off_most, off_max, near = sb("off_most", [P, 1]), sb("off_max", [1, 1]), sb("near", [1, 1], i32)

        end_idx = [sb(f"end_idx{b}", [P, E_TILES, 2], i32) for b in range(RING)]
        dst_row = [sb(f"dst_row{b}", [P, E_STEP], i32) for b in range(RING)]
        src_in = [sb(f"src_in{b}", [P, E_TILES, SRC_ROW]) for b in range(RING)]
        dst_in = [sb(f"dst_in{b}", [P, E_TILES, ROW]) for b in range(RING)]
        ends_norm = [sb(f"ends_norm{b}", [P, 2 * E_TILES, H]) for b in range(2)]
        ends_t, feat_t = sb("ends_t", [P, 2 * E_STEP]), sb("feat_t", [FEAT, E_STEP])
        hidden_e, msg, sums = sb("hidden_e", [P, E_STEP]), sb("msg", [P, E_STEP]), [sb(f"sums{b}", [P, E_TILES, H]) for b in range(RING)]
        equal = [sb(f"equal{b}", [P, E_TILES, P]) for b in range(RING)]
        junk = sb("junk", [P, E_TILES, P])
        earlier, own_off = sb("earlier", [P, E_TILES]), sb("own_off", [P, E_TILES])
        row_off = sb("row_off", [P, E_TILES])
        table_row = [sb(f"table_row{b}", [P, E_TILES], i32) for b in range(RING)]

        x_in = [sb(f"x_in{b}", [P, N_TILES, ROW]) for b in range(2)]
        agg_in = [sb(f"agg_in{b}", [P, N_TILES, H]) for b in range(2)]
        x_norm = [sb(f"x_norm{b}", [P, N_TILES, H]) for b in range(2)]
        x_beta = [sb(f"x_beta{b}", [P, N_TILES, H]) for b in range(RING)]
        h_t, hidden_n = sb("h_t", [P, N_STEP]), sb("hidden_n", [P, N_STEP])
        y, scaled = sb("y", [P, N_TILES, H]), sb("scaled", [P, N_TILES, H])
        y_out = [sb(f"y_out{b}", [P, N_TILES, H]) for b in range(2)]

        NS = 3 * N_TILES
        stats = sb("stats", [P, NS, 6])
        s_add, s_sub, s_m2, s_m2s, s_sq, var = (
            sb(n, [P, NS]) for n in ("s_add", "s_sub", "s_m2", "s_m2s", "s_sq", "var"))
        guess = sb("guess", [P, NS], i32)
        root = [sb(f"root{n}", [P, NS]) for n in range(NEWTON)]
        root_a, root_b = sb("root_a", [P, NS]), sb("root_b", [P, NS])
        mean = [sb(f"mean{b}", [P, NS]) for b in range(2)]
        rstd = [sb(f"rstd{b}", [P, NS]) for b in range(2)]
        minus = [sb(f"minus{b}", [P, NS]) for b in range(2)]

        ps_t = pb("ps_t", [P, N_STEP])
        ps_hid = pb("ps_hid", [P, N_STEP])
        ps_upd = pb("ps_upd", [P, N_STEP])
        ps_e = pb("ps_e", [P, E_STEP])
        ps_f = pb("ps_f", [P, E_STEP])

        sp_passed, pool_passed = sem("sp_passed"), sem("pool_passed")
        consts_loaded, weights_loaded = sem("consts_loaded"), sem("weights_loaded")
        zeros_made, zero_first, zero_rest = sem("zeros_made"), sem("zero_first"), sem("zero_rest")
        near_known = sem("near_known")
        off_most_ready, off_row_ready = sem("off_most_ready"), sem("off_row_ready")
        weights_multiplied, weights_copied = sem("weights_multiplied"), sem("weights_copied")
        setup_ops, setup_ready, bias_spread = sem("setup_ops"), sem("setup_ready"), sem("bias_spread")
        parts_ready, parts_transposed, parts_copied = sem("parts_ready"), sem("parts_transposed"), sem("parts_copied")
        edge_loaded = [sem(f"edge_loaded{b}") for b in range(RING)]
        gathered = [sem(f"gathered{b}") for b in range(RING)]
        x_loaded = [sem(f"x_loaded{b}") for b in range(2)]
        agg_loaded = [sem(f"agg_loaded{b}") for b in range(2)]
        stored = [sem(f"stored{b}") for b in range(2)]
        feat_joined, ends_norm_ready = sem("feat_joined"), sem("ends_norm_ready")
        ends_transposed, ends_copied = sem("ends_transposed"), sem("ends_copied")
        hidden_e_summed, hidden_e_ready = sem("hidden_e_summed"), sem("hidden_e_ready")
        msg_summed, msg_ready = sem("msg_summed"), sem("msg_ready")
        equal_ready, rows_ready, row_ops = sem("equal_ready"), sem("rows_ready"), sem("row_ops")
        sums_summed, sums_ready = sem("sums_summed"), sem("sums_ready")
        scattered = sem("scattered")
        x_beta_ready, x_norm_ready = sem("x_beta_ready"), sem("x_norm_ready")
        x_transposed, x_copied = sem("x_transposed"), sem("x_copied")
        hidden_n_summed, hidden_n_ready = sem("hidden_n_summed"), sem("hidden_n_ready")
        update_summed, y_ready = sem("update_summed"), sem("y_ready")
        scaled_ready, out_ready = sem("scaled_ready"), sem("out_ready")
        stat_ops, rstd_ready = sem("stat_ops"), sem("rstd_ready")

        block = ctx.enter_context(nc.Block())

        def near_flag(eng):
            eng.wait_ge(near_known, 1)
            return eng.value_load(near[0:1, 0:1], min_val=0, max_val=1)

        N_WEIGHTS = 16

        @block.sync
        def _(sp):
            sp.dma_start(dst_all[:, :], dst_place.rearrange("(p j) -> p j", p=P)).then_inc(consts_loaded, 16)
            sp.dma_start(const[:, :], consts).then_inc(consts_loaded, 16)
            loads = (
                (w_src[:, :], mW1[0:H, :]), (w_dst[:, :], mW1[H:2 * H, :]),
                (w_feat[0:1, :], mW1[2 * H + EDGE_DIM + 1:2 * H + EDGE_DIM + 2, :]),
                (w_feat[1:1 + EDGE_DIM + 1, :], mW1[2 * H:2 * H + EDGE_DIM + 1, :]),
                (w_node[:, :], uW1[0:H, :]), (w_agg[:, :], uW1[H:2 * H, :]), (w_msg[:, :], mW2),
                (w_out[:, :], uW2), (mb1_col[:, :], mb1.rearrange("(p o) -> p o", o=1)),
                (ub1_col[:, :], ub1.rearrange("(p o) -> p o", o=1)),
                (mb2_col[:, :], mb2.rearrange("(p o) -> p o", o=1)),
                (w_coord_col[:, :], uW1[2 * H:2 * H + 1, :].rearrange("o n -> n o")),
                (bias_rest[0:1, 1, 0, :], ub2.rearrange("(o n) -> o n", o=1)),
                (gamma_b[:, 0, :], gamma.rearrange("(o n) -> o n", o=1).broadcast_to([P, H])),
                (beta_b[:, 0, :], beta.rearrange("(o n) -> o n", o=1).broadcast_to([P, H])),
                (coord[:, :, :], node_vec.rearrange("(s p j) -> p s j", p=P, j=N_TILES)))
            assert len(loads) == N_WEIGHTS
            for dst, source in loads:
                sp.dma_start(dst, source).then_inc(weights_loaded, 16)

            def load_edges(s):
                b = s.slot
                wait_apart(sp, gathered[b], s.fills4 * 32 * E_TILES, sp_passed)
                wait_apart(sp, rows_ready, s.n - RING + 1, sp_passed)
                wait_apart(sp, ends_transposed, s.n - RING + 1, sp_passed)
                sp.dma_start(end_idx[b][:, :, :].rearrange("p t c -> p (t c)"), ends_v[s.n]).then_inc(edge_loaded[b], 16)
                sp.dma_start(dst_row[b][:, :], dst_v[bass.ds(s.n, 1), :].broadcast_to([P, E_STEP])).then_inc(edge_loaded[b], 16)
                sp.dma_start(src_in[b][:, :, 1:1 + EDGE_DIM], attr_v[s.n]).then_inc(edge_loaded[b], 16)

            def body(it):
                if isinstance(it.n, int) and it.n == 0:
                    for s in (it.edge(0), it.edge(1)):
                        if s:
                            load_edges(s)
                if s := it.edge(2):
                    load_edges(s)
                if k := it.node(1):
                    b = k.half
                    wait_apart(sp, x_norm_ready, k.n - 1, sp_passed)
                    wait_apart(sp, x_beta_ready, k.n - 1, sp_passed)
                    sp.dma_start(x_in[b][:, :, :].rearrange("p j f -> p (j f)"), rows_v[k.n]).then_inc(x_loaded[b], 16)
                if k := it.node(0):
                    b = k.half
                    reach = k.n + 2 if it.mode == WHOLE else EDGE_STEPS
                    wait_apart(sp, scattered, 16 * E_TILES * (min(reach, EDGE_STEPS) if isinstance(reach, int) else reach), sp_passed)
                    wait_apart(sp, hidden_n_summed, k.n - 1, sp_passed)
                    sp.dma_start(agg_in[b][:, :, :].rearrange("p j f -> p (j f)"), table_v[k.n]).then_inc(agg_loaded[b], 16)
                if k := it.node(-3):
                    b = k.half
                    wait_apart(sp, out_ready, k.n + 1, sp_passed)
                    sp.dma_start(out_v[k.n], y_out[b][:, :, :].rearrange("p j f -> p (j f)")).then_inc(stored[b], 16)

            flag = near_flag(sp)
            with sp.If(flag > 0):
                run_pipeline(sp, WHOLE, body)
            with sp.Else():
                run_pipeline(sp, EDGES_ONLY, body)
                run_pipeline(sp, NODES_ONLY, body)
            for b in range(2):
                sp.wait_ge(stored[b], 16 * ((NODE_STEPS + 1 - b) // 2))

        @block.gpsimd
        def _(pool):
            nc.gpsimd.memset(zeros[:, :], 0.0).then_inc(zeros_made, 1)

            def gather(s, t, side, dst):
                nc.gpsimd.indirect_dma_start(
                    out=dst, out_offset=None, in_=rows,
                    in_offset=bass.IndirectOffsetOnAxis(ap=end_idx[s.slot][:, t, side:side + 1], axis=0),
                ).then_inc(gathered[s.slot], 16)

            def body(it):
                new, old = it.edge(0), it.edge(-SCATTER_LAG)
                if new:
                    wait_apart(pool, edge_loaded[new.slot], (new.fills4 + 1) * 48, pool_passed)
                    wait_apart(pool, ends_norm_ready, new.n - RING + 1, pool_passed)
                    wait_apart(pool, ends_transposed, new.n - RING + 1, pool_passed)
                for t in range(E_TILES):
                    if new:
                        gather(new, t, 0, src_in[new.slot][:, t, 1 + EDGE_DIM:SRC_ROW])
                        gather(new, t, 1, dst_in[new.slot][:, t, :])
                    if old:
                        if t == 0:
                            wait_apart(pool, sums_ready, old.n + 1, pool_passed)
                            wait_apart(pool, rows_ready, old.n + 1, pool_passed)
                            if isinstance(old.n, int) and old.n == 0:
                                pool.wait_ge(zero_first, 16 * (ZERO_FIRST + 1))
                            if isinstance(old.n, int) and old.n == 2:
                                pool.wait_ge(zero_rest, 16 * (ZERO_DMAS - ZERO_FIRST))
                        wait_apart(pool, scattered, 16 * (E_TILES * old.n + t), pool_passed)
                        nc.gpsimd.indirect_dma_start(
                            out=table, out_offset=bass.IndirectOffsetOnAxis(ap=table_row[old.slot][:, t:t + 1], axis=0),
                            in_=sums[old.slot][:, t, :], in_offset=None, compute_op=ALU.add,
                        ).then_inc(scattered, 16)

            flag = near_flag(pool)
            with pool.If(flag > 0):
                run_pipeline(pool, WHOLE, body)
            with pool.Else():
                run_pipeline(pool, EDGES_ONLY, body)
            pool.wait_ge(scattered, 16 * E_TILES * EDGE_STEPS)

        @block.tensor
        def _(pe):
            def cols(t):
                return slice(t * P, (t + 1) * P)

            pe.wait_ge(consts_loaded, 32)
            pe.wait_ge(off_most_ready, 1)
            nc.tensor.transpose(ps_f[0:1, 0:P], off_most[:, :], ident).then_inc(off_row_ready, 1)
            pe.wait_ge(weights_loaded, 16 * N_WEIGHTS)
            nc.tensor.transpose(ps_e[:, 0:P], w_msg[:, :], ident).then_inc(weights_multiplied, 1)
            pe.wait_ge(weights_copied, 1)
            nc.tensor.matmul(ps_hid[:, 0:P], w_msg_t[:, :], w_agg[:, :], start=True, stop=True)
            nc.tensor.matmul(ps_upd[0:1, 0:P], mb2_col[:, :], w_agg[:, :], start=True, stop=True).then_inc(weights_multiplied, 1)
            pe.wait_ge(parts_ready, 1)
            for g in range(PART_GROUPS):
                if g >= 2:
                    pe.wait_ge(parts_copied, g - 1)
                bank = (ps_t[0:N_PARTS, 0:E_STEP] if g % 2 == 0 else ps_t[0:N_PARTS, E_STEP:N_STEP]).bitcast(bf16)
                for j in range(N_TILES):
                    if g == 0:
                        last = nc.tensor.transpose(bank[:, cols(j)], wc_cols[:, j, :, :, :].rearrange("p j a w -> p (j a w)"), ident_b[:, :])
                    elif (k := (g - 1) * N_TILES + j) < NODE_STEPS:
                        last = nc.tensor.transpose(bank[:, cols(j)], coord_part[:, k, :, :, :].rearrange("p j a w -> p (j a w)"), ident_b[:, :])
                last.then_inc(parts_transposed, 1)
            pe.wait_ge(parts_copied, PART_GROUPS)
            pe.wait_ge(setup_ready, 1)
            pe.wait_ge(bias_spread, 1)

            def body(it):
                k, e, old = it.node(0), it.edge(-1), it.edge(-2)
                if k:
                    pe.wait_ge(x_norm_ready, k.n + 1)
                    wait(pe, x_copied, k.n)
                    wait(pe, ends_copied, it.edges_upto(-2))
                    for j in range(N_TILES):
                        last = nc.tensor.transpose(ps_t[:, cols(j)], x_norm[k.half][:, j, :], ident)
                    last.then_inc(x_transposed, 1)
                if old:
                    pe.wait_ge(hidden_e_ready, old.n + 1)
                    for t in range(E_TILES):
                        nc.tensor.matmul(ps_e[:, cols(t)], ones_rows[:, :], bias_rows[:, 0, :], start=True, stop=False)
                        last = nc.tensor.matmul(ps_e[:, cols(t)], hidden_e[:, cols(t)], w_fold[:, :], start=False, stop=True)
                    last.then_inc(msg_summed, 1)
                if e:
                    pe.wait_ge(ends_norm_ready, e.n + 1)
                    wait(pe, ends_copied, e.n)
                    wait(pe, x_copied, it.nodes_upto(0))
                    for t in range(2 * E_TILES):
                        nc.tensor.transpose(ps_t[:, cols(t)], ends_norm[e.half][:, t, :], ident)
                    pe.wait_ge(edge_loaded[e.slot], (e.fills4 + 1) * 48)
                    pe.wait_ge(gathered[e.slot], (e.fills4 + 1) * 32 * E_TILES)
                    pe.wait_ge(feat_joined, e.n + 1)
                    wait(pe, sums_ready, e.n - 1)
                    for t in range(E_TILES):
                        last = nc.tensor.transpose(ps_f[:, cols(t)], src_in[e.slot][:, t, 0:P], ident)
                    last.then_inc(ends_transposed, 1)
                if k:
                    pe.wait_ge(x_copied, k.n + 1)
                    wait(pe, hidden_n_ready, k.n)
                    pe.wait_ge(agg_loaded[k.half], 16 * (k.fills2 + 1))
                    for j in range(N_TILES):
                        if j % E_TILES == 0:
                            bank = slice(j * P, j * P + E_STEP)
                            nc.tensor.matmul(ps_hid[:, bank], w_node[:, :], h_t[:, bank], start=True, stop=False)
                        nc.tensor.matmul(ps_hid[:, cols(j)], wc_rows[:, j, :], coord_t[:, k.n, :], start=False, stop=False)
                        last = nc.tensor.matmul(ps_hid[:, cols(j)], agg_in[k.half][:, j, :], ident, is_transpose=True,
                                                start=False, stop=j % E_TILES == E_TILES - 1)
                    last.then_inc(hidden_n_summed, 1)
                if e:
                    pe.wait_ge(ends_copied, e.n + 1)
                    wait(pe, msg_ready, e.n)
                    nc.tensor.matmul(ps_e[:, :], w_src[:, :], ends_t[:, 0:E_STEP], start=True, stop=False)
                    nc.tensor.matmul(ps_e[:, :], w_dst[:, :], ends_t[:, E_STEP:], start=False, stop=False)
                    nc.tensor.matmul(ps_e[:, :], w_feat[:, :], feat_t[:, :], start=False, stop=True).then_inc(hidden_e_summed, 1)
                if old:
                    pe.wait_ge(msg_ready, old.n + 1)
                    pe.wait_ge(equal_ready, old.n + 1)
                    wait(pe, ends_copied, it.edges_upto(-1))
                    for t in range(E_TILES):
                        last = nc.tensor.matmul(ps_f[:, cols(t)], equal[old.slot][:, t, :], msg[:, cols(t)], start=True, stop=True)
                    last.then_inc(sums_summed, 1)
                if k:
                    pe.wait_ge(hidden_n_ready, k.n + 1)
                    wait(pe, y_ready, k.n)
                    for j in range(N_TILES):
                        nc.tensor.matmul(ps_upd[:, cols(j)], ones_rows[:, :], bias_rows[:, 1, :], start=True, stop=False)
                        last = nc.tensor.matmul(ps_upd[:, cols(j)], hidden_n[:, cols(j)], w_out[:, :], start=False, stop=True)
                    last.then_inc(update_summed, 1)

            flag = near_flag(pe)
            with pe.If(flag > 0):
                run_pipeline(pe, WHOLE, body)
            with pe.Else():
                run_pipeline(pe, EDGES_ONLY, body)
                run_pipeline(pe, NODES_ONLY, body)

        @block.scalar
        def _(act):
            act.wait_ge(zeros_made, 1)

            def clear(first, rows_each, done):
                act.dma_start(table[first:first + P * rows_each, :].rearrange("(p r) f -> p (r f)", p=P),
                              zeros[:, 0:rows_each * H]).then_inc(done, 16)

            tail = ZERO_DMAS * ZERO_ROWS
            clear(tail, (TABLE_ROWS - tail) // P, zero_first)
            for z in range(ZERO_DMAS):
                clear(z * ZERO_ROWS, ZERO_ROWS // P, zero_first if z < ZERO_FIRST else zero_rest)

            act.wait_ge(weights_multiplied, 1)
            nc.scalar.activation(w_msg_t[:, :], ps_e[:, 0:P], ACT.Copy).then_inc(weights_copied, 1)
            act.wait_ge(weights_multiplied, 2)
            nc.scalar.activation(w_fold[:, :], ps_hid[:, 0:P], ACT.Copy)
            nc.scalar.activation(bias_rest[0:1, 0, 0, :], ps_upd[0:1, 0:P], ACT.Copy).then_inc(weights_copied, 1)
            for g in range(PART_GROUPS):
                act.wait_ge(parts_transposed, g + 1)
                bank = (ps_t[0:N_PARTS, 0:E_STEP] if g % 2 == 0 else ps_t[0:N_PARTS, E_STEP:N_STEP]).bitcast(bf16)
                if g == 0:
                    dst, n = wc_rows[:, :, :], N_TILES
                else:
                    n = min(N_TILES, NODE_STEPS - (g - 1) * N_TILES)
                    dst = coord_t[:, (g - 1) * N_TILES:(g - 1) * N_TILES + n, :]
                nc.scalar.activation(dst.rearrange("q j p -> q (j p)"), bank[:, 0:n * P], ACT.Copy).then_inc(parts_copied, 1)
            act.wait_ge(setup_ready, 1)
            for w in range(3):
                last = nc.scalar.activation(bias_rows[32 * w:32 * w + 1, :, :], bias_part[0:1, :, w, :], ACT.Copy)
            last.then_inc(bias_spread, 1)

            def body(it):
                k, e, old, new, nxt = it.node(0), it.edge(-1), it.edge(-2), it.edge(0), it.node(1)
                if k:
                    act.wait_ge(x_transposed, k.n + 1)
                    wait(act, hidden_n_summed, k.n)
                    nc.scalar.activation(h_t[:, :], ps_t[:, :], ACT.Relu).then_inc(x_copied, 1)
                if old:
                    act.wait_ge(msg_summed, old.n + 1)
                    wait(act, sums_summed, old.n)
                    nc.scalar.activation(msg[:, :], ps_e[:, :], ACT.Copy).then_inc(msg_ready, 1)
                if e:
                    act.wait_ge(ends_transposed, e.n + 1)
                    wait(act, hidden_e_summed, e.n)
                    nc.scalar.activation(ends_t[:, :], ps_t[:, :], ACT.Relu)
                    nc.scalar.activation(feat_t[:, :], ps_f[0:FEAT, :], ACT.Copy).then_inc(ends_copied, 1)
                if k:
                    act.wait_ge(hidden_n_summed, k.n + 1)
                    wait(act, update_summed, k.n)
                    nc.scalar.activation(hidden_n[:, :], ps_hid[:, :], ACT.Silu, bias=ub1_col[:, :]).then_inc(hidden_n_ready, 1)
                if e:
                    act.wait_ge(hidden_e_summed, e.n + 1)
                    wait(act, msg_summed, e.n)
                    nc.scalar.activation(hidden_e[:, :], ps_e[:, :], ACT.Silu, bias=mb1_col[:, :]).then_inc(hidden_e_ready, 1)
                if old:
                    act.wait_ge(sums_summed, old.n + 1)
                    wait(act, scattered, 16 * E_TILES * (old.n - RING + 1))
                    nc.scalar.activation(sums[old.slot][:, :, :].rearrange("p t f -> p (t f)"), ps_f[:, :], ACT.Copy).then_inc(sums_ready, 1)
                if new or nxt:
                    act.wait_ge(rstd_ready, it.stats_before() + 1)
                b = it.phase % 2
                if nxt:
                    act.wait_ge(x_loaded[nxt.half], 16 * (nxt.fills2 + 1))
                    wait(act, y_ready, nxt.n - 1)
                    wait(act, x_transposed, nxt.n - 1)
                    for j in range(N_TILES):
                        c = 2 * E_TILES + j
                        last = nc.scalar.activation(x_norm[nxt.half][:, j, :], x_in[nxt.half][:, j, 1:], ACT.Identity,
                                                    bias=minus[b][:, c:c + 1], scale=rstd[b][:, c:c + 1])
                    last.then_inc(x_norm_ready, 1)
                if new:
                    act.wait_ge(gathered[new.slot], (new.fills4 + 1) * 32 * E_TILES)
                    wait(act, ends_transposed, new.n - 1)
                    for c in range(2 * E_TILES):
                        t = c % E_TILES
                        source = src_in[new.slot][:, t, FEAT:] if c < E_TILES else dst_in[new.slot][:, t, 1:]
                        last = nc.scalar.activation(ends_norm[new.half][:, c, :], source, ACT.Identity,
                                                    bias=minus[b][:, c:c + 1], scale=rstd[b][:, c:c + 1])
                    last.then_inc(ends_norm_ready, 1)

            flag = near_flag(act)
            with act.If(flag > 0):
                run_pipeline(act, WHOLE, body)
            with act.Else():
                run_pipeline(act, EDGES_ONLY, body)
                run_pipeline(act, NODES_ONLY, body)

        STAT_OPS = 15

        @block.vector
        def _(dve):
            V = nc.vector

            dve.wait_ge(consts_loaded, 32)
            V.tensor_tensor(off_place[:, :], dst_all[:, :], place, ALU.subtract).then_inc(setup_ops, 1)
            dve.wait_ge(setup_ops, 1)
            V.tensor_tensor(off_square[:, :], off_place[:, :], off_place[:, :], ALU.mult).then_inc(setup_ops, 1)
            dve.wait_ge(setup_ops, 2)
            V.tensor_reduce(off_most[:, :], off_square[:, :], AX.X, ALU.max).then_inc(off_most_ready, 1)
            V.tensor_copy(ident_b[:, :], ident)
            V.memset(bias_rows[:, :, :], 0.0)
            V.memset(ones_rows[:, :], 1.0)
            V.memset(wc_cols[:, :, :, :, :], 0.0).then_inc(setup_ops, 1)
            dve.wait_ge(off_row_ready, 1)
            V.tensor_reduce(off_max[:, :], ps_f[0:1, 0:P], AX.X, ALU.max).then_inc(setup_ops, 1)
            dve.wait_ge(setup_ops, 4)
            V.tensor_scalar(near[:, :], off_max[:, :], float(NEAR) ** 2, None, ALU.is_le).then_inc(near_known, 1)

            dve.wait_ge(weights_loaded, 16 * N_WEIGHTS)
            done = 4
            for part in range(3):
                c_from, w_from = (coord, w_coord_col[:, :]) if part == 0 else (coord_rest, wc_rest[:, part - 1:part])
                V.tensor_copy(wc_part[:, part:part + 1], w_from)
                V.tensor_copy(coord_part[:, :, :, part, :],
                              c_from[:, :, :].rearrange("p s (j o) -> p (s j) o", o=1).broadcast_to([P, NODE_STEPS * N_TILES, 3])
                              .rearrange("p (s j) w -> p s j w", j=N_TILES)).then_inc(setup_ops, 1)
                done += 1
                dve.wait_ge(setup_ops, done)
                if part < 2:
                    V.tensor_tensor(wc_rest[:, part:part + 1], w_from, wc_part[:, part:part + 1], ALU.subtract)
                    V.tensor_tensor(coord_rest[:, :, :], c_from[:, :, :], coord_part[:, :, :, part, 0], ALU.subtract).then_inc(setup_ops, 1)
                    done += 1
                    dve.wait_ge(setup_ops, done)
            for j in range(N_TILES):
                last = V.tensor_copy(wc_cols[:, j, j, :, :], wc_part[:, :].rearrange("p (o w) -> p o w", o=1).broadcast_to([P, 3, 3]))
            last.then_inc(parts_ready, 1)
            dve.wait_ge(weights_copied, 2)
            for part in range(3):
                V.tensor_copy(bias_part[:, :, part, :], bias_rest[:, :, part, :]).then_inc(setup_ops if part < 2 else setup_ready, 1)
                if part < 2:
                    done += 1
                    dve.wait_ge(setup_ops, done)
                    V.tensor_tensor(bias_rest[:, :, part + 1, :], bias_rest[:, :, part, :], bias_part[:, :, part, :],
                                    ALU.subtract).then_inc(setup_ops, 1)
                    done += 1
                    dve.wait_ge(setup_ops, done)

            def body(it):
                new, nxt, prev = it.edge(0), it.node(1), it.node(-1)
                if not (new or nxt or prev):
                    return
                b = it.phase % 2
                base = it.stats_before() * STAT_OPS
                lo = 0 if new else 2 * E_TILES if nxt else 2 * E_TILES + N_TILES
                hi = 2 * E_TILES + 2 * N_TILES if prev else 2 * E_TILES + N_TILES if nxt else 2 * E_TILES
                at = slice(lo, hi)

                if prev:
                    dve.wait_ge(update_summed, prev.n + 1)
                    dve.wait_ge(x_norm_ready, prev.n + 1)
                    V.scalar_tensor_tensor(y[:, :, :], x_norm[prev.half][:, :, :], 0.0,
                                           ps_upd[:, :].rearrange("p (j f) -> p j f", f=H), ALU.max, ALU.add).then_inc(y_ready, 1)
                if new:
                    dve.wait_ge(gathered[new.slot], (new.fills4 + 1) * 32 * E_TILES)
                    V.tensor_copy(src_in[new.slot][:, :, 0:1], dst_in[new.slot][:, :, 0:1]).then_inc(feat_joined, 1)
                    for t in range(E_TILES):
                        last = V.bn_stats(stats[:, t, :], src_in[new.slot][:, t, FEAT:])
                        last = V.bn_stats(stats[:, E_TILES + t, :], dst_in[new.slot][:, t, 1:])
                if nxt:
                    dve.wait_ge(x_loaded[nxt.half], 16 * (nxt.fills2 + 1))
                    for j in range(N_TILES):
                        last = V.bn_stats(stats[:, 2 * E_TILES + j, :], x_in[nxt.half][:, j, 1:])
                if prev:
                    dve.wait_ge(y_ready, prev.n + 1)
                    for j in range(N_TILES):
                        last = V.bn_stats(stats[:, 2 * E_TILES + N_TILES + j, :], y[:, j, :])
                last.then_inc(stat_ops, 1)
                dve.wait_ge(stat_ops, base + 1)

                V.tensor_tensor(s_add[:, at], stats[:, at, 1], stats[:, at, 4], ALU.add)
                V.tensor_tensor(s_sub[:, at], stats[:, at, 1], stats[:, at, 4], ALU.subtract)
                V.tensor_tensor(s_m2[:, at], stats[:, at, 2], stats[:, at, 5], ALU.add).then_inc(stat_ops, 1)
                if new:
                    dve.wait_ge(edge_loaded[new.slot], (new.fills4 + 1) * 48)
                    wait(dve, sums_summed, new.n - RING + 1)
                    V.tensor_tensor(equal[new.slot][:, :, :], dst_row[new.slot][:, :].rearrange("p (j t) -> p t j", t=E_TILES),
                                    end_idx[new.slot][:, :, 1:2].broadcast_to([P, E_TILES, P]), ALU.is_equal).then_inc(equal_ready, 1)
                dve.wait_ge(stat_ops, base + 2)
                wait(dve, ends_norm_ready, it.edges_upto(-2))
                wait(dve, x_norm_ready, it.nodes_upto(-1))
                V.scalar_tensor_tensor(s_sq[:, at], s_sub[:, at], 0.25, s_sub[:, at], ALU.mult, ALU.mult)
                V.tensor_scalar(mean[b][:, at], s_add[:, at], 0.5, None, ALU.mult)
                V.tensor_scalar(s_m2s[:, at], s_m2[:, at], 1.0 / H, EPS, ALU.mult, ALU.add).then_inc(stat_ops, 1)
                if new:
                    dve.wait_ge(equal_ready, new.n + 1)
                    for t in range(2):
                        V.tensor_tensor_reduce(out=junk[:, t, :], in0=equal[new.slot][:, t, :], in1=lower, scale=1.0, scalar=0.0,
                                               op0=ALU.mult, op1=ALU.add, accum_out=earlier[:, t:t + 1])
                dve.wait_ge(stat_ops, base + 3)
                V.tensor_tensor(var[:, at], s_m2s[:, at], s_sq[:, at], ALU.add).then_inc(stat_ops, 1)
                if new:
                    for t in range(2, E_TILES):
                        last = V.tensor_tensor_reduce(out=junk[:, t, :], in0=equal[new.slot][:, t, :], in1=lower, scale=1.0, scalar=0.0,
                                                      op0=ALU.mult, op1=ALU.add, accum_out=earlier[:, t:t + 1])
                    V.tensor_scalar(own_off[:, :], end_idx[new.slot][:, :, 1], dummy_row, None, ALU.subtract).then_inc(row_ops, 1)
                dve.wait_ge(stat_ops, base + 4)
                V.tensor_scalar(guess[:, at], var[:, at].bitcast(i32), 1, None, ALU.logical_shift_right).then_inc(stat_ops, 1)
                if new:
                    dve.wait_ge(row_ops, 2 * new.n + 1)
                    wait(dve, scattered, 16 * E_TILES * (new.n - RING + 1))
                    V.scalar_tensor_tensor(row_off[:, :], earlier[:, :], 0.5, own_off[:, :], ALU.is_lt, ALU.mult).then_inc(row_ops, 1)
                dve.wait_ge(stat_ops, base + 5)
                V.tensor_scalar(root[0][:, at].bitcast(i32), guess[:, at], -1, MAGIC, ALU.mult, ALU.add).then_inc(stat_ops, 1)
                if new:
                    dve.wait_ge(row_ops, 2 * new.n + 2)
                    V.tensor_scalar(table_row[new.slot][:, :], row_off[:, :], dummy_row, None, ALU.add).then_inc(rows_ready, 1)
                op = 6
                for n in range(NEWTON):
                    result = root[n + 1] if n < NEWTON - 1 else rstd[b]
                    dve.wait_ge(stat_ops, base + op)
                    V.tensor_tensor(root_a[:, at], root[n][:, at], root[n][:, at], ALU.mult).then_inc(stat_ops, 1)
                    dve.wait_ge(stat_ops, base + op + 1)
                    V.scalar_tensor_tensor(root_b[:, at], root_a[:, at], -0.5, var[:, at], ALU.mult, ALU.mult).then_inc(stat_ops, 1)
                    if nxt and n == 0:
                        wait(dve, out_ready, nxt.n - RING + 1)
                        V.tensor_tensor(x_beta[nxt.slot][:, :, :], x_in[nxt.half][:, :, 1:], beta_b[:, :, :].broadcast_to([P, N_TILES, H]),
                                        ALU.add).then_inc(x_beta_ready, 1)
                    dve.wait_ge(stat_ops, base + op + 2)
                    V.scalar_tensor_tensor(result[:, at], root_b[:, at], 1.5, root[n][:, at], ALU.add, ALU.mult).then_inc(stat_ops, 1)
                    op += 3
                dve.wait_ge(stat_ops, base + op)
                V.scalar_tensor_tensor(minus[b][:, at], mean[b][:, at], -1.0, rstd[b][:, at], ALU.mult, ALU.mult).then_inc(rstd_ready, 1)
                assert op == STAT_OPS
                if prev:
                    for j in range(N_TILES):
                        c = 2 * E_TILES + N_TILES + j
                        last = V.scalar_tensor_tensor(scaled[:, j, :], y[:, j, :], mean[b][:, c:c + 1], gamma_b[:, 0, :],
                                                      ALU.subtract, ALU.mult)
                    last.then_inc(scaled_ready, 1)
                    dve.wait_ge(scaled_ready, prev.n + 1)
                    dve.wait_ge(x_beta_ready, prev.n + 1)
                    wait(dve, stored[prev.half], 16 * prev.fills2)
                    for j in range(N_TILES):
                        c = 2 * E_TILES + N_TILES + j
                        last = V.scalar_tensor_tensor(y_out[prev.half][:, j, :], scaled[:, j, :], rstd[b][:, c:c + 1],
                                                      x_beta[prev.slot][:, j, :], ALU.mult, ALU.add)
                    last.then_inc(out_ready, 1)

            flag = near_flag(dve)
            with dve.If(flag > 0):
                run_pipeline(dve, WHOLE, body)
            with dve.Else():
                run_pipeline(dve, EDGES_ONLY, body)
                run_pipeline(dve, NODES_ONLY, body)


def kernel(x, src, dst, edge_attr_32, node_vec, L0_gnn_mW1, L0_gnn_mb1, L0_gnn_mW2, L0_gnn_mb2, L0_gnn_uW1,
           L0_gnn_ub1, L0_gnn_uW2, L0_gnn_ub2, L0_gnn_ln_gamma, L0_gnn_ln_beta):
    import numpy as np
    import concourse.bacc as bacc
    from concourse.bass_utils import run_bass_kernel_spmd

    x, node_vec, src, dst, attr = (np.asarray(a) for a in (x, node_vec, src, dst, edge_attr_32))
    vec = np.zeros(NODES_PAD, node_vec.dtype)
    vec[:NODES] = node_vec
    rows = np.zeros((NODES_PAD, ROW), x.dtype)
    rows[:NODES, 1:] = x
    rows[:NODES, 0] = node_vec
    ends = np.full((EDGES_PAD, 2), NODES, src.dtype)
    ends[:EDGES, 0] = src
    ends[:EDGES, 1] = dst
    dst_place = np.full(EDGES_PAD, NODES, dst.dtype)
    dst_place[:EDGES] = dst
    attr_pad = np.zeros((EDGES_PAD, EDGE_DIM), attr.dtype)
    attr_pad[:EDGES] = attr
    consts = np.zeros((P, C_COLS), np.float32)
    consts[:, C_IDENT:C_IDENT + P] = np.eye(P)
    consts[:, C_LOWER:C_LOWER + P] = np.tri(P, k=-1)
    consts[:, C_DUMMY] = DUMMY + np.arange(P)
    consts[:, C_PLACE:] = (np.arange(EDGES_PAD) * (NODES // EDGES)).reshape(P, EDGE_COLS)

    arrays = {"rows": rows, "ends": ends, "dst": dst_place, "attr": attr_pad, "node_vec": vec,
              "mW1": L0_gnn_mW1, "mb1": L0_gnn_mb1, "mW2": L0_gnn_mW2, "mb2": L0_gnn_mb2,
              "uW1": L0_gnn_uW1, "ub1": L0_gnn_ub1, "uW2": L0_gnn_uW2, "ub2": L0_gnn_ub2,
              "gamma": L0_gnn_ln_gamma, "beta": L0_gnn_ln_beta, "consts": consts}
    nc = bacc.Bacc("TRN2", target_bir_lowering=False, num_devices=1)
    arrays = {f"in_{n}": np.ascontiguousarray(a) for n, a in arrays.items()}
    args = [nc.dram_tensor(n, a.shape, mybir.dt.from_np(a.dtype), kind="ExternalInput").ap() for n, a in arrays.items()]
    out = nc.dram_tensor("out", (NODES_PAD, H), mybir.dt.float32, kind="ExternalOutput").ap()
    gnn_layer(nc, *args, out)
    result = run_bass_kernel_spmd(nc, [arrays], core_ids=[0])
    return result.results[0]["out"][:NODES]
```

```python
from contextlib import ExitStack

import concourse.bass as bass
from concourse import mybir

P = 128
H = 128
EDGE_DIM = 32
NODES = 50000
EDGES = 25000
EPS = 1e-5

E_TILES = 4
E_STEP = E_TILES * P
EDGE_STEPS = -(-EDGES // E_STEP)
EDGES_PAD = EDGE_STEPS * E_STEP
N_TILES = 8
N_STEP = N_TILES * P
NODE_STEPS = -(-NODES // N_STEP)
NODES_PAD = NODE_STEPS * N_STEP
DUMMY = NODES_PAD
TABLE_ROWS = NODES_PAD + P

ROW = 1 + H
FEAT = 1 + EDGE_DIM + 1
SRC_ROW = 1 + EDGE_DIM + ROW

RING = 4
NEAR = 1024
SCATTER_LAG = 5
NODE_LAG = 6
X_ON_VECTOR = 3
X_TILES_AT = (4, 6, 8)[:X_ON_VECTOR]
X_EARLY = 2
N_PARTS = 9 * N_TILES
PART_GROUPS = 1 + -(-NODE_STEPS // N_TILES)
MAGIC = 0x5F3759DF

C_IDENT, C_LOWER, C_DUMMY, C_PLACE = 0, P, 2 * P, 2 * P + 1
EDGE_COLS = EDGES_PAD // P
C_COLS = C_PLACE + EDGE_COLS

WHOLE, EDGES_ONLY, NODES_ONLY = "whole", "edges", "nodes"


def wait(eng, semaphore, count):
    if isinstance(count, int) and count <= 0:
        return
    eng.wait_ge(semaphore, count)


def wait_apart(eng, semaphore, count, passed):
    if isinstance(count, int) and count <= 0:
        return
    eng.wait_ge(semaphore, count)
    eng.sem_inc(passed, 1)


class Step:

    def __init__(self, n, phase, quarter):
        self.n = n
        self.slot = phase % RING
        self.fills4 = quarter + phase // RING
        self.half = phase % 2
        self.fills2 = 2 * quarter + phase // 2


class Iteration:

    def __init__(self, mode, phase, quarter):
        self.mode = mode
        self.phase, self.quarter = phase, quarter
        self.n = RING * quarter + phase
        self.edges, self.nodes = mode != NODES_ONLY, mode != EDGES_ONLY
        self.lag = NODE_LAG if mode == WHOLE else 2

    def _step(self, shift, steps, present):
        n = self.n + shift
        if not present or (isinstance(n, int) and not 0 <= n < steps):
            return None
        return Step(n, self.phase + shift, self.quarter)

    def edge(self, shift):
        return self._step(shift, EDGE_STEPS, self.edges)

    def node(self, shift):
        return self._step(shift - self.lag, NODE_STEPS, self.nodes)

    def clearing(self, shift):
        return self._step(shift, NODE_STEPS, self.edges)

    def edges_upto(self, shift):
        if not self.edges:
            return EDGE_STEPS
        n = self.n + shift + 1
        return min(max(n, 0), EDGE_STEPS) if isinstance(n, int) else n

    def nodes_upto(self, shift):
        if not self.nodes:
            return 0
        n = self.n - self.lag + shift + 1
        return min(max(n, 0), NODE_STEPS) if isinstance(n, int) else n

    def stats_before(self):
        return self.n + (EDGE_STEPS if self.mode == NODES_ONLY else 0)


PIPELINES = {WHOLE: (NODE_LAG + 4, EDGE_STEPS - 2, NODE_STEPS + NODE_LAG + 3),
             EDGES_ONLY: (SCATTER_LAG + 4, EDGE_STEPS - 2, EDGE_STEPS + SCATTER_LAG),
             NODES_ONLY: (8, NODE_STEPS - 1, NODE_STEPS + 5)}


def run_pipeline(eng, mode, body):
    first, last, total = PIPELINES[mode]
    first = -(-first // RING)
    last = last // RING
    for n in range(first * RING):
        body(Iteration(mode, n % RING, n // RING))
    with eng.Fori(first, last) as quarter:
        for phase in range(RING):
            body(Iteration(mode, phase, quarter))
    for n in range(last * RING, total):
        body(Iteration(mode, n % RING, n // RING))


def gnn_layer(nc, rows, ends, dst_place, attr, node_vec, mW1, mb1, mW2, mb2, uW1, ub1, uW2, ub2,
              gamma, beta, consts, out):
    f32, bf16, i32 = mybir.dt.float32, mybir.dt.bfloat16, mybir.dt.int32
    ALU, ACT, AX = mybir.AluOpType, mybir.ActivationFunctionType, mybir.AxisListType

    ends_v = ends.rearrange("(s p t) c -> s p (t c)", p=P, t=E_TILES)
    dst_v = dst_place.rearrange("(s n) -> s n", n=E_STEP)
    attr_v = attr.rearrange("(s p t) f -> s p t f", p=P, t=E_TILES)
    rows_v = rows.rearrange("(s p j) f -> s p (j f)", p=P, j=N_TILES)
    out_v = out.rearrange("(s p j) f -> s p (j f)", p=P, j=N_TILES)
    table = nc.dram_tensor("table", (TABLE_ROWS, H), f32, kind="Internal").ap()
    table_v = table[0:NODES_PAD, :].rearrange("(s p j) f -> s p (j f)", p=P, j=N_TILES)

    ctx = ExitStack()
    with ctx:
        def sb(name, shape, dt=f32):
            return ctx.enter_context(nc.sbuf_tensor(name, shape, dt))

        def pb(name, shape, dt=f32):
            return ctx.enter_context(nc.psum_tensor(name, shape, dt))

        def sem(name):
            return ctx.enter_context(nc.semaphore(name))

        const = sb("const_sb", [P, C_COLS])
        ident, lower = const[:, C_IDENT:C_IDENT + P], const[:, C_LOWER:C_LOWER + P]
        dummy_row, place = const[:, C_DUMMY:C_DUMMY + 1], const[:, C_PLACE:C_PLACE + EDGE_COLS]
        ident_b = sb("ident_b", [P, P], bf16)
        w_src, w_dst, w_feat = sb("w_src", [P, H]), sb("w_dst", [P, H]), sb("w_feat", [FEAT, H])
        w_node, w_agg, w_msg, w_msg_t = sb("w_node", [P, H]), sb("w_agg", [P, H]), sb("w_msg", [P, H]), sb("w_msg_t", [P, H])
        w_fold, w_out = sb("w_fold", [P, H]), sb("w_out", [P, H])
        mb1_col, ub1_col, mb2_col, w_coord_col = (sb(n, [P, 1]) for n in ("mb1_col", "ub1_col", "mb2_col", "w_coord_col"))
        gamma_b, beta_b = sb("gamma_b", [P, 1, H]), sb("beta_b", [P, 1, H])
        bias_rest = sb("bias_rest", [1, 2, 3, H])
        bias_part = sb("bias_part", [1, 2, 3, H], bf16)
        bias_rows = sb("bias_rows", [96, 2, H], bf16)
        ones_rows = sb("ones_rows", [96, P], bf16)
        coord = sb("coord", [P, NODE_STEPS, N_TILES])
        coord_rest = sb("coord_rest", [P, NODE_STEPS, N_TILES])
        coord_part = sb("coord_part", [P, NODE_STEPS, N_TILES, 3, 3], bf16)
        wc_part = sb("wc_part", [P, 3], bf16)
        wc_rest = sb("wc_rest", [P, 3])
        wc_cols = sb("wc_cols", [P, N_TILES, N_TILES, 3, 3], bf16)
        wc_rows = sb("wc_rows", [N_PARTS, N_TILES, H], bf16)
        coord_t = sb("coord_t", [N_PARTS, NODE_STEPS, P], bf16)
        zeros = sb("zeros", [P, N_TILES, H])
        dst_all = sb("dst_all", [P, EDGE_COLS], i32)
        off_place, off_square = sb("off_place", [P, EDGE_COLS]), sb("off_square", [P, EDGE_COLS])
        off_most, off_max, near = sb("off_most", [P, 1]), sb("off_max", [1, 1]), sb("near", [1, 1], i32)

        end_idx = [sb(f"end_idx{b}", [P, E_TILES, 2], i32) for b in range(RING)]
        dst_row = [sb(f"dst_row{b}", [P, E_STEP], i32) for b in range(RING)]
        src_in = [sb(f"src_in{b}", [P, E_TILES, SRC_ROW]) for b in range(RING)]
        dst_in = [sb(f"dst_in{b}", [P, E_TILES, ROW]) for b in range(RING)]
        ends_norm = [sb(f"ends_norm{b}", [P, 2 * E_TILES, H]) for b in range(2)]
        ends_t, feat_t = sb("ends_t", [P, 2 * E_STEP]), sb("feat_t", [FEAT, E_STEP])
        hidden_e, msg, sums = sb("hidden_e", [P, E_STEP]), sb("msg", [P, E_STEP]), [sb(f"sums{b}", [P, E_TILES, H]) for b in range(RING)]
        equal = [sb(f"equal{b}", [P, E_TILES, P]) for b in range(RING)]
        upto, own_off = sb("upto", [P, E_TILES]), sb("own_off", [P, E_TILES])
        row_off = sb("row_off", [P, E_TILES])
        table_row = [sb(f"table_row{b}", [P, E_TILES], i32) for b in range(RING)]

        x_in = [sb(f"x_in{b}", [P, N_TILES, ROW]) for b in range(RING)]
        agg_in = [sb(f"agg_in{b}", [P, N_TILES, H]) for b in range(2)]
        x_norm = [sb(f"x_norm{b}", [P, N_TILES, H]) for b in range(2)]
        x_beta = [sb(f"x_beta{b}", [P, N_TILES, H]) for b in range(2)]
        h_t = [sb(f"h_t{b}", [P, N_STEP]) for b in range(2)]
        hidden_n = sb("hidden_n", [P, N_STEP])
        y_norm = [sb(f"y_norm{b}", [P, N_TILES, H]) for b in range(2)]
        scaled = sb("scaled", [P, N_TILES, H])
        y_out = [sb(f"y_out{b}", [P, N_TILES, H]) for b in range(2)]

        NS = 3 * N_TILES
        stats = sb("stats", [P, NS, 6])
        s_add, s_sub, s_m2, s_m2s, s_sq, var = (
            sb(n, [P, NS]) for n in ("s_add", "s_sub", "s_m2", "s_m2s", "s_sq", "var"))
        guess, halley, root_a, root_b, root_c, root_d, newton_a, newton_b = (
            sb(n, [P, NS]) for n in ("guess", "halley", "root_a", "root_b", "root_c", "root_d", "newton_a", "newton_b"))
        rstd = [sb(f"rstd{b}", [P, NS]) for b in range(RING)]
        minus = [sb(f"minus{b}", [P, NS]) for b in range(RING)]

        ps_t = pb("ps_t", [P, N_STEP])
        ps_hid = pb("ps_hid", [P, N_STEP])
        ps_upd = pb("ps_upd", [P, N_STEP])
        ps_e = pb("ps_e", [P, E_STEP])
        ps_f = pb("ps_f", [P, E_STEP])

        sp_passed, pool_passed = sem("sp_passed"), sem("pool_passed")
        consts_loaded, weights_loaded = sem("consts_loaded"), sem("weights_loaded")
        zeros_made, dummies_cleared = sem("zeros_made"), sem("dummies_cleared")
        cleared = [sem(f"cleared{b}") for b in range(RING)]
        near_known = sem("near_known")
        off_most_ready, off_row_ready = sem("off_most_ready"), sem("off_row_ready")
        weights_multiplied, weights_copied = sem("weights_multiplied"), sem("weights_copied")
        setup_ops, setup_ready, bias_spread = sem("setup_ops"), sem("setup_ready"), sem("bias_spread")
        parts_ready, parts_transposed, parts_copied = sem("parts_ready"), sem("parts_transposed"), sem("parts_copied")
        edge_loaded = [sem(f"edge_loaded{b}") for b in range(RING)]
        gathered = [sem(f"gathered{b}") for b in range(RING)]
        x_loaded = [sem(f"x_loaded{b}") for b in range(RING)]
        agg_loaded = [sem(f"agg_loaded{b}") for b in range(2)]
        stored = [sem(f"stored{b}") for b in range(2)]
        feat_joined, ends_norm_ready = sem("feat_joined"), sem("ends_norm_ready")
        ends_transposed, ends_copied = sem("ends_transposed"), sem("ends_copied")
        hidden_e_summed, hidden_e_ready = sem("hidden_e_summed"), sem("hidden_e_ready")
        msg_summed, msg_ready = sem("msg_summed"), sem("msg_ready")
        equal_ready, rows_ready, row_ops = sem("equal_ready"), sem("rows_ready"), sem("row_ops")
        sums_summed, sums_ready = sem("sums_summed"), sem("sums_ready")
        scattered = sem("scattered")
        x_beta_ready, x_norm_ready, x_norm_rest_ready = sem("x_beta_ready"), sem("x_norm_ready"), sem("x_norm_rest_ready")
        x_transposed, x_copied = sem("x_transposed"), sem("x_copied")
        hidden_n_summed, hidden_n_ready = sem("hidden_n_summed"), sem("hidden_n_ready")
        update_summed, y_norm_ready = sem("update_summed"), sem("y_norm_ready")
        scaled_ready, out_ready = sem("scaled_ready"), sem("out_ready")
        stat_ops, rstd_ready = sem("stat_ops"), sem("rstd_ready")

        block = ctx.enter_context(nc.Block())

        def near_flag(eng):
            eng.wait_ge(near_known, 1)
            return eng.value_load(near[0:1, 0:1], min_val=0, max_val=1)

        N_WEIGHTS = 16

        @block.sync
        def _(sp):
            sp.dma_start(dst_all[:, :], dst_place.rearrange("(p j) -> p j", p=P)).then_inc(consts_loaded, 16)
            sp.dma_start(const[:, :], consts).then_inc(consts_loaded, 16)

            def load_edges(s):
                b = s.slot
                wait_apart(sp, gathered[b], s.fills4 * 32 * E_TILES, sp_passed)
                wait_apart(sp, rows_ready, s.n - RING + 1, sp_passed)
                wait_apart(sp, ends_transposed, s.n - RING + 1, sp_passed)
                sp.dma_start(end_idx[b][:, :, :].rearrange("p t c -> p (t c)"), ends_v[s.n]).then_inc(edge_loaded[b], 16)
                sp.dma_start(dst_row[b][:, :], dst_v[bass.ds(s.n, 1), :].broadcast_to([P, E_STEP])).then_inc(edge_loaded[b], 16)
                sp.dma_start(src_in[b][:, :, 1:1 + EDGE_DIM], attr_v[s.n]).then_inc(edge_loaded[b], 16)

            def load_nodes(k):
                b = k.slot
                wait_apart(sp, x_norm_ready, k.n - RING + 1, sp_passed)
                wait_apart(sp, x_norm_rest_ready, k.n - RING + 1, sp_passed)
                wait_apart(sp, x_beta_ready, k.n - RING + 1, sp_passed)
                sp.dma_start(x_in[b][:, :, :].rearrange("p j f -> p (j f)"), rows_v[k.n]).then_inc(x_loaded[b], 16)

            def clear(block):
                wait_apart(sp, cleared[block.slot], 16 * block.fills4, sp_passed)
                sp.dma_start(table_v[block.n], zeros[:, :, :].rearrange("p j f -> p (j f)")).then_inc(cleared[block.slot], 16)

            def body(it):
                if isinstance(it.n, int) and it.n == 0:
                    for s in (it.edge(0), it.edge(1)):
                        if s:
                            load_edges(s)
                    for k in (it.node(n) for n in range(3)):
                        if k:
                            load_nodes(k)
                    if it.edges:
                        sp.wait_ge(zeros_made, 1)
                        sp.dma_start(table[DUMMY:TABLE_ROWS, :], zeros[:, 0, :]).then_inc(dummies_cleared, 16)
                    if it.mode == EDGES_ONLY:
                        with sp.Fori(0, NODE_STEPS // RING) as quarter:
                            for phase in range(RING):
                                clear(Step(RING * quarter + phase, phase, quarter))
                        for n in range(NODE_STEPS // RING * RING, NODE_STEPS):
                            clear(Step(n, n % RING, n // RING))
                if it.mode == WHOLE and (block := it.clearing(0)):
                    clear(block)
                if k := it.node(0):
                    b = k.half
                    reach = k.n + 2 if it.mode == WHOLE else EDGE_STEPS
                    wait_apart(sp, scattered, 16 * E_TILES * (min(reach, EDGE_STEPS) if isinstance(reach, int) else reach), sp_passed)
                    wait_apart(sp, hidden_n_summed, k.n - 1, sp_passed)
                    sp.dma_start(agg_in[b][:, :, :].rearrange("p j f -> p (j f)"), table_v[k.n]).then_inc(agg_loaded[b], 16)
                if k := it.node(-3):
                    b = k.half
                    wait_apart(sp, out_ready, k.n + 1, sp_passed)
                    sp.dma_start(out_v[k.n], y_out[b][:, :, :].rearrange("p j f -> p (j f)")).then_inc(stored[b], 16)
                if k := it.node(3):
                    load_nodes(k)
                if s := it.edge(2):
                    load_edges(s)

            flag = near_flag(sp)
            with sp.If(flag > 0):
                run_pipeline(sp, WHOLE, body)
            with sp.Else():
                run_pipeline(sp, EDGES_ONLY, body)
                run_pipeline(sp, NODES_ONLY, body)
            for b in range(2):
                sp.wait_ge(stored[b], 16 * ((NODE_STEPS + 1 - b) // 2))

        @block.gpsimd
        def _(pool):
            nc.gpsimd.memset(zeros[:, :, :], 0.0).then_inc(zeros_made, 1)

            def gather(s, t, side, dst):
                nc.gpsimd.indirect_dma_start(
                    out=dst, out_offset=None, in_=rows,
                    in_offset=bass.IndirectOffsetOnAxis(ap=end_idx[s.slot][:, t, side:side + 1], axis=0),
                ).then_inc(gathered[s.slot], 16)

            def body(it):
                new, old = it.edge(0), it.edge(-SCATTER_LAG)
                if new:
                    wait_apart(pool, edge_loaded[new.slot], (new.fills4 + 1) * 48, pool_passed)
                    wait_apart(pool, ends_norm_ready, new.n - RING + 1, pool_passed)
                    wait_apart(pool, ends_transposed, new.n - RING + 1, pool_passed)
                for t in range(E_TILES):
                    if old:
                        if t == 0:
                            wait_apart(pool, sums_ready, old.n + 1, pool_passed)
                            wait_apart(pool, rows_ready, old.n + 1, pool_passed)
                            if isinstance(old.n, int) and old.n == 0:
                                pool.wait_ge(dummies_cleared, 16)
                            if it.mode == WHOLE:
                                if near_clear := it.clearing(1 - SCATTER_LAG):
                                    wait_apart(pool, cleared[near_clear.slot], 16 * (near_clear.fills4 + 1), pool_passed)
                                if isinstance(old.n, int) and old.n == 0:
                                    pool.wait_ge(cleared[0], 16)
                            elif isinstance(old.n, int) and old.n == 0:
                                for b in range(RING):
                                    pool.wait_ge(cleared[b], 16 * len(range(b, NODE_STEPS, RING)))
                        wait_apart(pool, scattered, 16 * (E_TILES * old.n + t), pool_passed)
                        nc.gpsimd.indirect_dma_start(
                            out=table, out_offset=bass.IndirectOffsetOnAxis(ap=table_row[old.slot][:, t:t + 1], axis=0),
                            in_=sums[old.slot][:, t, :], in_offset=None, compute_op=ALU.add,
                        ).then_inc(scattered, 16)
                    if new:
                        gather(new, t, 0, src_in[new.slot][:, t, 1 + EDGE_DIM:SRC_ROW])
                        gather(new, t, 1, dst_in[new.slot][:, t, :])

            flag = near_flag(pool)
            with pool.If(flag > 0):
                run_pipeline(pool, WHOLE, body)
            with pool.Else():
                run_pipeline(pool, EDGES_ONLY, body)
            pool.wait_ge(scattered, 16 * E_TILES * EDGE_STEPS)

        @block.tensor
        def _(pe):
            def cols(t):
                return slice(t * P, (t + 1) * P)

            pe.wait_ge(consts_loaded, 32)
            pe.wait_ge(off_most_ready, 1)
            nc.tensor.transpose(ps_f[0:1, 0:P], off_most[:, :], ident).then_inc(off_row_ready, 1)
            pe.wait_ge(weights_loaded, 16 * N_WEIGHTS)
            nc.tensor.transpose(ps_e[:, 0:P], w_msg[:, :], ident).then_inc(weights_multiplied, 1)
            pe.wait_ge(weights_copied, 1)
            nc.tensor.matmul(ps_hid[:, 0:P], w_msg_t[:, :], w_agg[:, :], start=True, stop=True)
            nc.tensor.matmul(ps_upd[0:1, 0:P], mb2_col[:, :], w_agg[:, :], start=True, stop=True).then_inc(weights_multiplied, 1)
            pe.wait_ge(parts_ready, 1)
            for g in range(PART_GROUPS):
                if g >= 2:
                    pe.wait_ge(parts_copied, g - 1)
                bank = (ps_t[0:N_PARTS, 0:E_STEP] if g % 2 == 0 else ps_t[0:N_PARTS, E_STEP:N_STEP]).bitcast(bf16)
                for j in range(N_TILES):
                    if g == 0:
                        last = nc.tensor.transpose(bank[:, cols(j)], wc_cols[:, j, :, :, :].rearrange("p j a w -> p (j a w)"), ident_b[:, :])
                    elif (k := (g - 1) * N_TILES + j) < NODE_STEPS:
                        last = nc.tensor.transpose(bank[:, cols(j)], coord_part[:, k, :, :, :].rearrange("p j a w -> p (j a w)"), ident_b[:, :])
                last.then_inc(parts_transposed, 1)
            pe.wait_ge(parts_copied, PART_GROUPS)
            pe.wait_ge(setup_ready, 1)
            pe.wait_ge(bias_spread, 1)

            def body(it):
                nxt, k, own, e, old = it.node(1), it.node(0), it.edge(-1), it.edge(-2), it.edge(-3)
                if k:
                    pe.wait_ge(x_copied, k.n + 1)
                    wait(pe, hidden_n_ready, k.n)
                    pe.wait_ge(agg_loaded[k.half], 16 * (k.fills2 + 1))
                    for j in range(N_TILES):
                        if j % E_TILES == 0:
                            bank = slice(j * P, j * P + E_STEP)
                            nc.tensor.matmul(ps_hid[:, bank], w_node[:, :], h_t[k.half][:, bank], start=True, stop=False)
                        nc.tensor.matmul(ps_hid[:, cols(j)], wc_rows[:, j, :], coord_t[:, k.n, :], start=False, stop=False)
                        last = nc.tensor.matmul(ps_hid[:, cols(j)], agg_in[k.half][:, j, :], ident, is_transpose=True,
                                                start=False, stop=j % E_TILES == E_TILES - 1)
                    last.then_inc(hidden_n_summed, 1)
                if old:
                    pe.wait_ge(msg_ready, old.n + 1)
                    pe.wait_ge(equal_ready, old.n + 1)
                    wait(pe, ends_copied, it.edges_upto(-2))
                    for t in range(E_TILES):
                        last = nc.tensor.matmul(ps_f[:, cols(t)], equal[old.slot][:, t, :], msg[:, cols(t)], start=True, stop=True)
                    last.then_inc(sums_summed, 1)
                if e:
                    pe.wait_ge(ends_copied, e.n + 1)
                    wait(pe, msg_ready, e.n)
                    nc.tensor.matmul(ps_e[:, :], w_src[:, :], ends_t[:, 0:E_STEP], start=True, stop=False)
                    nc.tensor.matmul(ps_e[:, :], w_dst[:, :], ends_t[:, E_STEP:], start=False, stop=False)
                    nc.tensor.matmul(ps_e[:, :], w_feat[:, :], feat_t[:, :], start=False, stop=True).then_inc(hidden_e_summed, 1)
                if nxt:
                    pe.wait_ge(x_norm_ready, nxt.n + 1)
                    pe.wait_ge(x_norm_rest_ready, nxt.n + 1)
                    wait(pe, x_copied, nxt.n)
                    wait(pe, ends_copied, it.edges_upto(-2))
                    for j in range(N_TILES):
                        last = nc.tensor.transpose(ps_t[:, cols(j)], x_norm[nxt.half][:, j, :], ident)
                    last.then_inc(x_transposed, 1)
                if k:
                    pe.wait_ge(hidden_n_ready, k.n + 1)
                    for j in range(N_TILES):
                        if j % E_TILES == 0:
                            wait(pe, y_norm_ready, 2 * k.n - 1 + j // E_TILES)
                        nc.tensor.matmul(ps_upd[:, cols(j)], ones_rows[:, :], bias_rows[:, 1, :], start=True, stop=False)
                        nc.tensor.matmul(ps_upd[:, cols(j)], hidden_n[:, cols(j)], w_out[:, :], start=False, stop=False)
                        last = nc.tensor.matmul(ps_upd[:, cols(j)], h_t[k.half][:, cols(j)], ident, is_transpose=True, start=False, stop=True)
                        if j % E_TILES == E_TILES - 1:
                            last.then_inc(update_summed, 1)
                if e:
                    pe.wait_ge(hidden_e_ready, e.n + 1)
                    for t in range(E_TILES):
                        nc.tensor.matmul(ps_e[:, cols(t)], ones_rows[:, :], bias_rows[:, 0, :], start=True, stop=False)
                        last = nc.tensor.matmul(ps_e[:, cols(t)], hidden_e[:, cols(t)], w_fold[:, :], start=False, stop=True)
                    last.then_inc(msg_summed, 1)
                if own:
                    pe.wait_ge(ends_norm_ready, own.n + 1)
                    wait(pe, ends_copied, own.n)
                    wait(pe, x_copied, it.nodes_upto(1))
                    for t in range(2 * E_TILES):
                        nc.tensor.transpose(ps_t[:, cols(t)], ends_norm[own.half][:, t, :], ident)
                    pe.wait_ge(edge_loaded[own.slot], (own.fills4 + 1) * 48)
                    pe.wait_ge(gathered[own.slot], (own.fills4 + 1) * 32 * E_TILES)
                    pe.wait_ge(feat_joined, own.n + 1)
                    wait(pe, sums_ready, it.edges_upto(-3))
                    for t in range(E_TILES):
                        last = nc.tensor.transpose(ps_f[:, cols(t)], src_in[own.slot][:, t, 0:P], ident)
                    last.then_inc(ends_transposed, 1)

            flag = near_flag(pe)
            with pe.If(flag > 0):
                run_pipeline(pe, WHOLE, body)
            with pe.Else():
                run_pipeline(pe, EDGES_ONLY, body)
                run_pipeline(pe, NODES_ONLY, body)

        @block.scalar
        def _(act):
            loads = (
                (w_src[:, :], mW1[0:H, :]), (w_dst[:, :], mW1[H:2 * H, :]),
                (w_feat[0:1, :], mW1[2 * H + EDGE_DIM + 1:2 * H + EDGE_DIM + 2, :]),
                (w_feat[1:1 + EDGE_DIM + 1, :], mW1[2 * H:2 * H + EDGE_DIM + 1, :]),
                (w_node[:, :], uW1[0:H, :]), (w_agg[:, :], uW1[H:2 * H, :]), (w_msg[:, :], mW2),
                (w_out[:, :], uW2), (mb1_col[:, :], mb1.rearrange("(p o) -> p o", o=1)),
                (ub1_col[:, :], ub1.rearrange("(p o) -> p o", o=1)),
                (mb2_col[:, :], mb2.rearrange("(p o) -> p o", o=1)),
                (w_coord_col[:, :], uW1[2 * H:2 * H + 1, :].rearrange("o n -> n o")),
                (bias_rest[0:1, 1, 0, :], ub2.rearrange("(o n) -> o n", o=1)),
                (gamma_b[:, 0, :], gamma.rearrange("(o n) -> o n", o=1).broadcast_to([P, H])),
                (beta_b[:, 0, :], beta.rearrange("(o n) -> o n", o=1).broadcast_to([P, H])),
                (coord[:, :, :], node_vec.rearrange("(s p j) -> p s j", p=P, j=N_TILES)))
            assert len(loads) == N_WEIGHTS
            for dst, source in loads:
                act.dma_start(dst, source).then_inc(weights_loaded, 16)

            act.wait_ge(weights_multiplied, 1)
            nc.scalar.activation(w_msg_t[:, :], ps_e[:, 0:P], ACT.Copy).then_inc(weights_copied, 1)
            act.wait_ge(weights_multiplied, 2)
            nc.scalar.activation(w_fold[:, :], ps_hid[:, 0:P], ACT.Copy)
            nc.scalar.activation(bias_rest[0:1, 0, 0, :], ps_upd[0:1, 0:P], ACT.Copy).then_inc(weights_copied, 1)
            for g in range(PART_GROUPS):
                act.wait_ge(parts_transposed, g + 1)
                bank = (ps_t[0:N_PARTS, 0:E_STEP] if g % 2 == 0 else ps_t[0:N_PARTS, E_STEP:N_STEP]).bitcast(bf16)
                if g == 0:
                    dst, n = wc_rows[:, :, :], N_TILES
                else:
                    n = min(N_TILES, NODE_STEPS - (g - 1) * N_TILES)
                    dst = coord_t[:, (g - 1) * N_TILES:(g - 1) * N_TILES + n, :]
                nc.scalar.activation(dst.rearrange("q j p -> q (j p)"), bank[:, 0:n * P], ACT.Copy).then_inc(parts_copied, 1)
            act.wait_ge(setup_ready, 1)
            for w in range(3):
                last = nc.scalar.activation(bias_rows[32 * w:32 * w + 1, :, :], bias_part[0:1, :, w, :], ACT.Copy)
            last.then_inc(bias_spread, 1)

            def body(it):
                nxt, near_nxt, k, prev = it.node(2), it.node(1), it.node(0), it.node(-1)
                own, e, old = it.edge(-1), it.edge(-2), it.edge(-3)
                now, was = it.phase, (it.phase - 1) % RING

                def norm(dst, source, c, slot):
                    return nc.scalar.activation(dst, source, ACT.Identity, bias=minus[slot][:, c:c + 1], scale=rstd[slot][:, c:c + 1])

                if own:
                    act.wait_ge(rstd_ready, it.stats_before())
                    act.wait_ge(gathered[own.slot], (own.fills4 + 1) * 32 * E_TILES)
                    wait(act, ends_transposed, own.n - 1)
                    for t in range(E_TILES):
                        norm(ends_norm[own.half][:, E_TILES + t, :], dst_in[own.slot][:, t, 1:], E_TILES + t, was)
                if old:
                    act.wait_ge(msg_summed, old.n + 1)
                    wait(act, sums_summed, old.n)
                    nc.scalar.activation(msg[:, :], ps_e[:, :], ACT.Copy).then_inc(msg_ready, 1)
                if e:
                    act.wait_ge(ends_transposed, e.n + 1)
                    wait(act, hidden_e_summed, e.n)
                    nc.scalar.activation(ends_t[:, :], ps_t[:, :], ACT.Relu)
                    nc.scalar.activation(feat_t[:, :], ps_f[0:FEAT, :], ACT.Copy).then_inc(ends_copied, 1)
                if near_nxt:
                    act.wait_ge(rstd_ready, it.stats_before())
                    act.wait_ge(x_loaded[near_nxt.slot], 16 * (near_nxt.fills4 + 1))
                    for j in range(X_EARLY, N_TILES - X_ON_VECTOR):
                        last = norm(x_norm[near_nxt.half][:, j, :], x_in[near_nxt.slot][:, j, 1:], 2 * E_TILES + j, was)
                    last.then_inc(x_norm_ready, 1)
                if k:
                    act.wait_ge(hidden_n_summed, k.n + 1)
                    wait(act, update_summed, 2 * k.n)
                    nc.scalar.activation(hidden_n[:, :], ps_hid[:, :], ACT.Silu, bias=ub1_col[:, :]).then_inc(hidden_n_ready, 1)
                if old:
                    act.wait_ge(sums_summed, old.n + 1)
                    wait(act, scattered, 16 * E_TILES * (old.n - RING + 1))
                    nc.scalar.activation(sums[old.slot][:, :, :].rearrange("p t f -> p (t f)"), ps_f[:, :], ACT.Copy).then_inc(sums_ready, 1)
                if prev:
                    act.wait_ge(rstd_ready, it.stats_before() + 1)
                    act.wait_ge(update_summed, 2 * prev.n + 2)
                    wait(act, scaled_ready, prev.n - 1)
                    for j in range(N_TILES):
                        last = norm(y_norm[prev.half][:, j, :], ps_upd[:, j * P:(j + 1) * P], 2 * E_TILES + N_TILES + j, now)
                        if j % E_TILES == E_TILES - 1:
                            last.then_inc(y_norm_ready, 1)
                if near_nxt:
                    act.wait_ge(x_transposed, near_nxt.n + 1)
                    wait(act, update_summed, 2 * near_nxt.n - 2)
                    nc.scalar.activation(h_t[near_nxt.half][:, :], ps_t[:, :], ACT.Relu).then_inc(x_copied, 1)
                if e:
                    act.wait_ge(hidden_e_summed, e.n + 1)
                    wait(act, msg_summed, e.n)
                    nc.scalar.activation(hidden_e[:, :], ps_e[:, :], ACT.Silu, bias=mb1_col[:, :]).then_inc(hidden_e_ready, 1)
                if own:
                    for t in range(E_TILES):
                        last = norm(ends_norm[own.half][:, t, :], src_in[own.slot][:, t, FEAT:], t, was)
                    last.then_inc(ends_norm_ready, 1)
                if nxt:
                    act.wait_ge(rstd_ready, it.stats_before() + 1)
                    act.wait_ge(x_loaded[nxt.slot], 16 * (nxt.fills4 + 1))
                    wait(act, x_transposed, nxt.n - 1)
                    for j in range(X_EARLY):
                        norm(x_norm[nxt.half][:, j, :], x_in[nxt.slot][:, j, 1:], 2 * E_TILES + j, now)

            flag = near_flag(act)
            with act.If(flag > 0):
                run_pipeline(act, WHOLE, body)
            with act.Else():
                run_pipeline(act, EDGES_ONLY, body)
                run_pipeline(act, NODES_ONLY, body)

        STAT_OPS = 13

        @block.vector
        def _(dve):
            V = nc.vector

            dve.wait_ge(consts_loaded, 32)
            V.tensor_tensor(off_place[:, :], dst_all[:, :], place, ALU.subtract).then_inc(setup_ops, 1)
            dve.wait_ge(setup_ops, 1)
            V.tensor_tensor(off_square[:, :], off_place[:, :], off_place[:, :], ALU.mult).then_inc(setup_ops, 1)
            dve.wait_ge(setup_ops, 2)
            V.tensor_reduce(off_most[:, :], off_square[:, :], AX.X, ALU.max).then_inc(off_most_ready, 1)
            V.tensor_copy(ident_b[:, :], ident)
            V.memset(bias_rows[:, :, :], 0.0)
            V.memset(ones_rows[:, :], 1.0)
            V.memset(wc_cols[:, :, :, :, :], 0.0).then_inc(setup_ops, 1)
            dve.wait_ge(off_row_ready, 1)
            V.tensor_reduce(off_max[:, :], ps_f[0:1, 0:P], AX.X, ALU.max).then_inc(setup_ops, 1)
            dve.wait_ge(setup_ops, 4)
            V.tensor_scalar(near[:, :], off_max[:, :], float(NEAR) ** 2, None, ALU.is_le).then_inc(near_known, 1)

            dve.wait_ge(weights_loaded, 16 * N_WEIGHTS)
            done = 4
            for part in range(3):
                c_from, w_from = (coord, w_coord_col[:, :]) if part == 0 else (coord_rest, wc_rest[:, part - 1:part])
                V.tensor_copy(wc_part[:, part:part + 1], w_from)
                V.tensor_copy(coord_part[:, :, :, part, :],
                              c_from[:, :, :].rearrange("p s (j o) -> p (s j) o", o=1).broadcast_to([P, NODE_STEPS * N_TILES, 3])
                              .rearrange("p (s j) w -> p s j w", j=N_TILES)).then_inc(setup_ops, 1)
                done += 1
                dve.wait_ge(setup_ops, done)
                if part < 2:
                    V.tensor_tensor(wc_rest[:, part:part + 1], w_from, wc_part[:, part:part + 1], ALU.subtract)
                    V.tensor_tensor(coord_rest[:, :, :], c_from[:, :, :], coord_part[:, :, :, part, 0], ALU.subtract).then_inc(setup_ops, 1)
                    done += 1
                    dve.wait_ge(setup_ops, done)
            for j in range(N_TILES):
                last = V.tensor_copy(wc_cols[:, j, j, :, :], wc_part[:, :].rearrange("p (o w) -> p o w", o=1).broadcast_to([P, 3, 3]))
            last.then_inc(parts_ready, 1)
            dve.wait_ge(weights_copied, 2)
            for part in range(3):
                V.tensor_copy(bias_part[:, :, part, :], bias_rest[:, :, part, :]).then_inc(setup_ops if part < 2 else setup_ready, 1)
                if part < 2:
                    done += 1
                    dve.wait_ge(setup_ops, done)
                    V.tensor_tensor(bias_rest[:, :, part + 1, :], bias_rest[:, :, part, :], bias_part[:, :, part, :],
                                    ALU.subtract).then_inc(setup_ops, 1)
                    done += 1
                    dve.wait_ge(setup_ops, done)

            def body(it):
                new, nxt, prev = it.edge(0), it.node(2), it.node(-1)
                own, near_nxt, done = it.edge(-2), it.node(1), it.node(-2)
                b, was = it.phase, (it.phase - 1) % RING
                HALF = N_TILES // 2

                def beside(n):
                    if own and n < E_TILES:
                        if n == 0:
                            dve.wait_ge(edge_loaded[own.slot], (own.fills4 + 1) * 48)
                            wait(dve, sums_summed, own.n - RING + 1)
                        last = V.scalar_tensor_tensor(
                            equal[own.slot][:, n, :], dst_row[own.slot][:, :].rearrange("p (j t) -> p t j", t=E_TILES)[:, n, :],
                            end_idx[own.slot][:, n, 1:2], lower, ALU.is_equal, ALU.mult, accum_out=upto[:, n:n + 1])
                        if n == E_TILES - 1:
                            last.then_inc(equal_ready, 1)
                            V.tensor_scalar(own_off[:, :], end_idx[own.slot][:, :, 1], dummy_row, None, ALU.subtract).then_inc(row_ops, 1)
                    if own and n == E_TILES + 1:
                        dve.wait_ge(row_ops, 2 * own.n + 1)
                        V.scalar_tensor_tensor(row_off[:, :], upto[:, :], 1.5, own_off[:, :], ALU.is_lt, ALU.mult).then_inc(row_ops, 1)
                    if own and n == E_TILES + 5:
                        dve.wait_ge(row_ops, 2 * own.n + 2)
                        wait(dve, scattered, 16 * E_TILES * (own.n - RING + 1))
                        V.tensor_scalar(table_row[own.slot][:, :], row_off[:, :], dummy_row, None, ALU.add).then_inc(rows_ready, 1)
                    if done and n in (12, 13):
                        part = slice(0, HALF) if n == 12 else slice(HALF, N_TILES)
                        dve.wait_ge(y_norm_ready, 2 * done.n + 2)
                        last = V.tensor_tensor(scaled[:, part, :], y_norm[done.half][:, part, :],
                                               gamma_b[:, :, :].broadcast_to([P, HALF, H]), ALU.mult)
                        if n == 13:
                            last.then_inc(scaled_ready, 1)
                    if done and n in (14, 15):
                        part = slice(0, HALF) if n == 14 else slice(HALF, N_TILES)
                        dve.wait_ge(scaled_ready, done.n + 1)
                        dve.wait_ge(x_beta_ready, done.n + 1)
                        wait(dve, stored[done.half], 16 * done.fills2)
                        last = V.tensor_tensor(y_out[done.half][:, part, :], scaled[:, part, :], x_beta[done.half][:, part, :], ALU.add)
                        if n == 15:
                            last.then_inc(out_ready, 1)
                    if near_nxt and n in X_TILES_AT:
                        j = N_TILES - X_ON_VECTOR + X_TILES_AT.index(n)
                        c = 2 * E_TILES + j
                        if n == X_TILES_AT[0]:
                            dve.wait_ge(rstd_ready, it.stats_before())
                            wait(dve, x_transposed, near_nxt.n - 1)
                        last = V.tensor_scalar(x_norm[near_nxt.half][:, j, :], x_in[near_nxt.slot][:, j, 1:],
                                               rstd[was][:, c:c + 1], minus[was][:, c:c + 1], ALU.mult, ALU.add)
                        if n == X_TILES_AT[-1]:
                            last.then_inc(x_norm_rest_ready, 1)
                    if prev and n in (16, 17):
                        part = slice(0, HALF) if n == 16 else slice(HALF, N_TILES)
                        wait(dve, out_ready, prev.n - 1)
                        last = V.tensor_tensor(x_beta[prev.half][:, part, :], x_in[prev.slot][:, part, 1:],
                                               beta_b[:, :, :].broadcast_to([P, HALF, H]), ALU.add)
                        if n == 17:
                            last.then_inc(x_beta_ready, 1)

                if not (new or nxt or prev):
                    for n in (16, 17, 12, 13, 14, 15, *range(12)):
                        beside(n)
                    return

                base = it.stats_before() * STAT_OPS
                lo = 0 if new else 2 * E_TILES if nxt else 2 * E_TILES + N_TILES
                hi = 2 * E_TILES + 2 * N_TILES if prev else 2 * E_TILES + N_TILES if nxt else 2 * E_TILES
                at = slice(lo, hi)
                for n in (16, 17):
                    beside(n)
                if nxt:
                    dve.wait_ge(x_loaded[nxt.slot], 16 * (nxt.fills4 + 1))
                    for j in range(N_TILES):
                        last = V.bn_stats(stats[:, 2 * E_TILES + j, :], x_in[nxt.slot][:, j, 1:])
                if new:
                    dve.wait_ge(gathered[new.slot], (new.fills4 + 1) * 32 * E_TILES)
                    V.tensor_copy(src_in[new.slot][:, :, 0:1], dst_in[new.slot][:, :, 0:1]).then_inc(feat_joined, 1)
                    for t in range(E_TILES):
                        V.bn_stats(stats[:, t, :], src_in[new.slot][:, t, FEAT:])
                        last = V.bn_stats(stats[:, E_TILES + t, :], dst_in[new.slot][:, t, 1:])
                for n in (12, 13, 14, 15):
                    beside(n)
                if prev:
                    for j in range(N_TILES):
                        if j % E_TILES == 0:
                            dve.wait_ge(update_summed, 2 * prev.n + 1 + j // E_TILES)
                        last = V.bn_stats(stats[:, 2 * E_TILES + N_TILES + j, :], ps_upd[:, j * P:(j + 1) * P])
                last.then_inc(stat_ops, 1)
                beside(0)
                dve.wait_ge(stat_ops, base + 1)
                V.tensor_tensor(s_sub[:, at], stats[:, at, 1], stats[:, at, 4], ALU.subtract)
                V.tensor_tensor(s_m2[:, at], stats[:, at, 2], stats[:, at, 5], ALU.add)
                V.tensor_tensor(s_add[:, at], stats[:, at, 1], stats[:, at, 4], ALU.add).then_inc(stat_ops, 1)
                beside(1)
                dve.wait_ge(stat_ops, base + 2)
                V.scalar_tensor_tensor(s_sq[:, at], s_sub[:, at], 0.25, s_sub[:, at], ALU.mult, ALU.mult)
                V.tensor_scalar(s_m2s[:, at], s_m2[:, at], 1.0 / H, EPS, ALU.mult, ALU.add).then_inc(stat_ops, 1)
                beside(2)
                dve.wait_ge(stat_ops, base + 3)
                V.tensor_tensor(var[:, at], s_m2s[:, at], s_sq[:, at], ALU.add).then_inc(stat_ops, 1)
                beside(3)
                dve.wait_ge(stat_ops, base + 4)
                V.tensor_scalar(guess[:, at].bitcast(i32), var[:, at].bitcast(i32), -0.5, MAGIC, ALU.mult, ALU.add).then_inc(stat_ops, 1)
                beside(4)
                dve.wait_ge(stat_ops, base + 5)
                V.tensor_tensor(root_a[:, at], guess[:, at], guess[:, at], ALU.mult).then_inc(stat_ops, 1)
                beside(5)
                dve.wait_ge(stat_ops, base + 6)
                V.tensor_tensor(root_b[:, at], root_a[:, at], var[:, at], ALU.mult).then_inc(stat_ops, 1)
                beside(6)
                dve.wait_ge(stat_ops, base + 7)
                V.tensor_scalar(root_c[:, at], root_b[:, at], 0.375, -1.25, ALU.mult, ALU.add).then_inc(stat_ops, 1)
                beside(7)
                dve.wait_ge(stat_ops, base + 8)
                V.tensor_tensor(root_d[:, at], root_c[:, at], root_b[:, at], ALU.mult).then_inc(stat_ops, 1)
                beside(8)
                dve.wait_ge(stat_ops, base + 9)
                V.scalar_tensor_tensor(halley[:, at], root_d[:, at], 1.875, guess[:, at], ALU.add, ALU.mult).then_inc(stat_ops, 1)
                beside(9)
                dve.wait_ge(stat_ops, base + 10)
                V.tensor_tensor(newton_a[:, at], halley[:, at], halley[:, at], ALU.mult).then_inc(stat_ops, 1)
                beside(10)
                dve.wait_ge(stat_ops, base + 11)
                V.scalar_tensor_tensor(newton_b[:, at], newton_a[:, at], -0.5, var[:, at], ALU.mult, ALU.mult).then_inc(stat_ops, 1)
                beside(11)
                dve.wait_ge(stat_ops, base + 12)
                wait(dve, ends_norm_ready, it.edges_upto(-RING))
                wait(dve, x_norm_ready, it.nodes_upto(-2))
                V.scalar_tensor_tensor(rstd[b][:, at], newton_b[:, at], 1.5, halley[:, at], ALU.add, ALU.mult).then_inc(stat_ops, 1)
                dve.wait_ge(stat_ops, base + STAT_OPS)
                V.scalar_tensor_tensor(minus[b][:, at], s_add[:, at], -0.5, rstd[b][:, at], ALU.mult, ALU.mult).then_inc(rstd_ready, 1)

            flag = near_flag(dve)
            with dve.If(flag > 0):
                run_pipeline(dve, WHOLE, body)
            with dve.Else():
                run_pipeline(dve, EDGES_ONLY, body)
                run_pipeline(dve, NODES_ONLY, body)


def kernel(x, src, dst, edge_attr_32, node_vec, L0_gnn_mW1, L0_gnn_mb1, L0_gnn_mW2, L0_gnn_mb2, L0_gnn_uW1,
           L0_gnn_ub1, L0_gnn_uW2, L0_gnn_ub2, L0_gnn_ln_gamma, L0_gnn_ln_beta):
    import numpy as np
    import concourse.bacc as bacc
    from concourse.bass_utils import run_bass_kernel_spmd

    x, node_vec, src, dst, attr = (np.asarray(a) for a in (x, node_vec, src, dst, edge_attr_32))
    vec = np.zeros(NODES_PAD, node_vec.dtype)
    vec[:NODES] = node_vec
    rows = np.zeros((NODES_PAD, ROW), x.dtype)
    rows[:NODES, 1:] = x
    rows[:NODES, 0] = node_vec
    ends = np.full((EDGES_PAD, 2), NODES, src.dtype)
    ends[:EDGES, 0] = src
    ends[:EDGES, 1] = dst
    dst_place = np.full(EDGES_PAD, NODES, dst.dtype)
    dst_place[:EDGES] = dst
    attr_pad = np.zeros((EDGES_PAD, EDGE_DIM), attr.dtype)
    attr_pad[:EDGES] = attr
    consts = np.zeros((P, C_COLS), np.float32)
    consts[:, C_IDENT:C_IDENT + P] = np.eye(P)
    consts[:, C_LOWER:C_LOWER + P] = np.tri(P)
    consts[:, C_DUMMY] = DUMMY + np.arange(P)
    consts[:, C_PLACE:] = (np.arange(EDGES_PAD) * (NODES // EDGES)).reshape(P, EDGE_COLS)

    arrays = {"rows": rows, "ends": ends, "dst": dst_place, "attr": attr_pad, "node_vec": vec,
              "mW1": L0_gnn_mW1, "mb1": L0_gnn_mb1, "mW2": L0_gnn_mW2, "mb2": L0_gnn_mb2,
              "uW1": L0_gnn_uW1, "ub1": L0_gnn_ub1, "uW2": L0_gnn_uW2, "ub2": L0_gnn_ub2,
              "gamma": L0_gnn_ln_gamma, "beta": L0_gnn_ln_beta, "consts": consts}
    nc = bacc.Bacc("TRN2", target_bir_lowering=False, num_devices=1)
    arrays = {f"in_{n}": np.ascontiguousarray(a) for n, a in arrays.items()}
    args = [nc.dram_tensor(n, a.shape, mybir.dt.from_np(a.dtype), kind="ExternalInput").ap() for n, a in arrays.items()]
    out = nc.dram_tensor("out", (NODES_PAD, H), mybir.dt.float32, kind="ExternalOutput").ap()
    gnn_layer(nc, *args, out)
    result = run_bass_kernel_spmd(nc, [arrays], core_ids=[0])
    return result.results[0]["out"][:NODES]
```

```python
from contextlib import ExitStack

import concourse.bass as bass
from concourse import mybir

P = 128
H = 128
EDGE_DIM = 32
NODES = 50000
EDGES = 25000
EPS = 1e-5

E_TILES = 4
E_STEP = E_TILES * P
EDGE_STEPS = -(-EDGES // E_STEP)
EDGES_PAD = EDGE_STEPS * E_STEP
N_TILES = 8
N_STEP = N_TILES * P
NODE_STEPS = -(-NODES // N_STEP)
NODES_PAD = NODE_STEPS * N_STEP
DUMMY = NODES_PAD
TABLE_ROWS = NODES_PAD + P

ROW = 1 + H
FEAT = 1 + EDGE_DIM + 1
SRC_ROW = 1 + EDGE_DIM + ROW

RING = 4
NEAR = 1024
EDGES_AHEAD, X_AHEAD = 2, 3
PIECES = 4
SCATTER_LAG = 5
NODE_LAG = 6
X_ON_VECTOR = 3
X_EARLY = 1
N_PARTS = 9 * N_TILES
PART_GROUPS = 1 + -(-NODE_STEPS // N_TILES)
MAGIC = 0x5F3759DF

C_IDENT, C_LOWER, C_DUMMY, C_PLACE = 0, P, 2 * P, 2 * P + 1
EDGE_COLS = EDGES_PAD // P
C_COLS = C_PLACE + EDGE_COLS

WHOLE, EDGES_ONLY, NODES_ONLY = "whole", "edges", "nodes"


def wait(eng, semaphore, count):
    if isinstance(count, int) and count <= 0:
        return
    eng.wait_ge(semaphore, count)


def wait_apart(eng, semaphore, count, passed):
    if isinstance(count, int) and count <= 0:
        return
    eng.wait_ge(semaphore, count)
    eng.sem_inc(passed, 1)


class Step:

    def __init__(self, n, phase, quarter):
        self.n = n
        self.slot = phase % RING
        self.fills4 = quarter + phase // RING
        self.half = phase % 2
        self.fills2 = 2 * quarter + phase // 2


class Iteration:

    def __init__(self, mode, phase, quarter):
        self.mode = mode
        self.phase, self.quarter = phase, quarter
        self.n = RING * quarter + phase
        self.edges, self.nodes = mode != NODES_ONLY, mode != EDGES_ONLY
        self.lag = NODE_LAG if mode == WHOLE else 2

    def _step(self, shift, steps, present):
        n = self.n + shift
        if not present or (isinstance(n, int) and not 0 <= n < steps):
            return None
        return Step(n, self.phase + shift, self.quarter)

    def edge(self, shift):
        return self._step(shift, EDGE_STEPS, self.edges)

    def node(self, shift):
        return self._step(shift - self.lag, NODE_STEPS, self.nodes)

    def clearing(self, shift):
        return self._step(shift, NODE_STEPS, self.edges)

    def edges_upto(self, shift):
        if not self.edges:
            return EDGE_STEPS
        n = self.n + shift + 1
        return min(max(n, 0), EDGE_STEPS) if isinstance(n, int) else n

    def nodes_upto(self, shift):
        if not self.nodes:
            return 0
        n = self.n - self.lag + shift + 1
        return min(max(n, 0), NODE_STEPS) if isinstance(n, int) else n

    def stats_before(self):
        return self.n + (EDGE_STEPS if self.mode == NODES_ONLY else 0)


PIPELINES = {WHOLE: (NODE_LAG + 4, EDGE_STEPS - 2, NODE_STEPS + NODE_LAG + 3),
             EDGES_ONLY: (SCATTER_LAG + 4, EDGE_STEPS - 2, EDGE_STEPS + SCATTER_LAG),
             NODES_ONLY: (8, NODE_STEPS - 1, NODE_STEPS + 5)}


def run_pipeline(eng, mode, body):
    first, last, total = PIPELINES[mode]
    first = -(-first // RING)
    last = last // RING
    for n in range(first * RING):
        body(Iteration(mode, n % RING, n // RING))
    with eng.Fori(first, last) as quarter:
        for phase in range(RING):
            body(Iteration(mode, phase, quarter))
    for n in range(last * RING, total):
        body(Iteration(mode, n % RING, n // RING))


def gnn_layer(nc, rows, ends, dst_place, attr, node_vec, mW1, mb1, mW2, mb2, uW1, ub1, uW2, ub2,
              gamma, beta, consts, out):
    f32, bf16, i32 = mybir.dt.float32, mybir.dt.bfloat16, mybir.dt.int32
    ALU, ACT, AX = mybir.AluOpType, mybir.ActivationFunctionType, mybir.AxisListType

    ends_v = ends.rearrange("(s p t) c -> s p (t c)", p=P, t=E_TILES)
    dst_v = dst_place.rearrange("(s n) -> s n", n=E_STEP)
    attr_v = attr.rearrange("(s p t) f -> s p t f", p=P, t=E_TILES)
    rows_v = rows.rearrange("(s p j) f -> s p j f", p=P, j=N_TILES)
    out_v = out.rearrange("(s p j) f -> s p j f", p=P, j=N_TILES)
    table = nc.dram_tensor("table", (TABLE_ROWS, H), f32, kind="Internal").ap()
    table_v = table[0:NODES_PAD, :].rearrange("(s p j) f -> s p j f", p=P, j=N_TILES)

    ctx = ExitStack()
    with ctx:
        def sb(name, shape, dt=f32):
            return ctx.enter_context(nc.sbuf_tensor(name, shape, dt))

        def pb(name, shape, dt=f32):
            return ctx.enter_context(nc.psum_tensor(name, shape, dt))

        def sem(name):
            return ctx.enter_context(nc.semaphore(name))

        const = sb("const_sb", [P, C_COLS])
        ident, lower = const[:, C_IDENT:C_IDENT + P], const[:, C_LOWER:C_LOWER + P]
        dummy_row, place = const[:, C_DUMMY:C_DUMMY + 1], const[:, C_PLACE:C_PLACE + EDGE_COLS]
        ident_b = sb("ident_b", [P, P], bf16)
        w_src, w_dst, w_feat = sb("w_src", [P, H]), sb("w_dst", [P, H]), sb("w_feat", [FEAT, H])
        w_node, w_agg, w_msg, w_msg_t = sb("w_node", [P, H]), sb("w_agg", [P, H]), sb("w_msg", [P, H]), sb("w_msg_t", [P, H])
        w_fold, w_out = sb("w_fold", [P, H]), sb("w_out", [P, H])
        mb1_col, ub1_col, mb2_col, w_coord_col = (sb(n, [P, 1]) for n in ("mb1_col", "ub1_col", "mb2_col", "w_coord_col"))
        gamma_b, beta_b = sb("gamma_b", [P, 1, H]), sb("beta_b", [P, 1, H])
        bias_rest = sb("bias_rest", [1, 2, 3, H])
        bias_part = sb("bias_part", [1, 2, 3, H], bf16)
        bias_rows = sb("bias_rows", [96, 2, H], bf16)
        ones_rows = sb("ones_rows", [96, P], bf16)
        coord = sb("coord", [P, NODE_STEPS, N_TILES])
        coord_rest = sb("coord_rest", [P, NODE_STEPS, N_TILES])
        coord_part = sb("coord_part", [P, NODE_STEPS, N_TILES, 3, 3], bf16)
        wc_part = sb("wc_part", [P, 3], bf16)
        wc_rest = sb("wc_rest", [P, 3])
        wc_cols = sb("wc_cols", [P, N_TILES, N_TILES, 3, 3], bf16)
        wc_rows = sb("wc_rows", [N_PARTS, N_TILES, H], bf16)
        coord_t = sb("coord_t", [N_PARTS, NODE_STEPS, P], bf16)
        zeros = sb("zeros", [P, N_TILES, H])
        dst_all = sb("dst_all", [P, EDGE_COLS], i32)
        off_place, off_square = sb("off_place", [P, EDGE_COLS]), sb("off_square", [P, EDGE_COLS])
        off_most, off_max, near = sb("off_most", [P, 1]), sb("off_max", [1, 1]), sb("near", [1, 1], i32)

        end_idx = [sb(f"end_idx{b}", [P, E_TILES, 2], i32) for b in range(RING)]
        dst_row = [sb(f"dst_row{b}", [P, E_STEP], i32) for b in range(RING)]
        src_in = [sb(f"src_in{b}", [P, E_TILES, SRC_ROW]) for b in range(RING)]
        dst_in = [sb(f"dst_in{b}", [P, E_TILES, ROW]) for b in range(RING)]
        ends_norm = [sb(f"ends_norm{b}", [P, 2 * E_TILES, H]) for b in range(2)]
        ends_t, feat_t = sb("ends_t", [P, 2 * E_STEP]), sb("feat_t", [FEAT, E_STEP])
        hidden_e, msg, sums = sb("hidden_e", [P, E_STEP]), sb("msg", [P, E_STEP]), [sb(f"sums{b}", [P, E_TILES, H]) for b in range(RING)]
        equal = [sb(f"equal{b}", [P, E_TILES, P]) for b in range(RING)]
        upto, repeats = sb("upto", [P, E_TILES]), sb("repeats", [P, E_TILES])
        table_row = [sb(f"table_row{b}", [P, E_TILES], i32) for b in range(RING)]

        x_in = [sb(f"x_in{b}", [P, N_TILES, ROW]) for b in range(RING)]
        agg_in = [sb(f"agg_in{b}", [P, N_TILES, H]) for b in range(2)]
        x_norm = [sb(f"x_norm{b}", [P, N_TILES, H]) for b in range(2)]
        x_beta = [sb(f"x_beta{b}", [P, N_TILES, H]) for b in range(2)]
        h_t = [sb(f"h_t{b}", [P, N_STEP]) for b in range(2)]
        hidden_n = sb("hidden_n", [P, N_STEP])
        y_norm = [sb(f"y_norm{b}", [P, N_TILES, H]) for b in range(2)]
        scaled = sb("scaled", [P, N_TILES, H])
        y_out = [sb(f"y_out{b}", [P, N_TILES, H]) for b in range(2)]

        NS = 3 * N_TILES
        stats = sb("stats", [P, NS, 6])
        s_add, s_sub, s_m2, s_m2s, s_sq, var = (
            sb(n, [P, NS]) for n in ("s_add", "s_sub", "s_m2", "s_m2s", "s_sq", "var"))
        guess, halley, root_a, root_b, root_c, root_d, newton_a, newton_b = (
            sb(n, [P, NS]) for n in ("guess", "halley", "root_a", "root_b", "root_c", "root_d", "newton_a", "newton_b"))
        rstd = [sb(f"rstd{b}", [P, NS]) for b in range(RING)]
        minus = [sb(f"minus{b}", [P, NS]) for b in range(RING)]

        ps_t = pb("ps_t", [P, N_STEP])
        ps_hid = pb("ps_hid", [P, N_STEP])
        ps_upd = pb("ps_upd", [P, N_STEP])
        ps_e = pb("ps_e", [P, E_STEP])
        ps_f = pb("ps_f", [P, E_STEP])

        sp_passed, pool_passed = sem("sp_passed"), sem("pool_passed")
        consts_loaded, fold_loaded = sem("consts_loaded"), sem("fold_loaded")
        weights_loaded, late_loaded = sem("weights_loaded"), sem("late_loaded")
        zeros_made, dummies_cleared = sem("zeros_made"), sem("dummies_cleared")
        cleared = [sem(f"cleared{b}") for b in range(RING)]
        near_known = sem("near_known")
        off_most_ready, off_row_ready = sem("off_most_ready"), sem("off_row_ready")
        weights_multiplied, weights_copied = sem("weights_multiplied"), sem("weights_copied")
        setup_ops, setup_ready, bias_spread = sem("setup_ops"), sem("setup_ready"), sem("bias_spread")
        parts_ready, parts_transposed, parts_copied = sem("parts_ready"), sem("parts_transposed"), sem("parts_copied")
        edge_loaded = [sem(f"edge_loaded{b}") for b in range(RING)]
        gathered = [sem(f"gathered{b}") for b in range(RING)]
        x_loaded = [sem(f"x_loaded{b}") for b in range(RING)]
        agg_loaded = [sem(f"agg_loaded{b}") for b in range(2)]
        stored = [sem(f"stored{b}") for b in range(2)]
        feat_joined, ends_norm_ready = sem("feat_joined"), sem("ends_norm_ready")
        ends_transposed, ends_copied = sem("ends_transposed"), sem("ends_copied")
        hidden_e_summed, hidden_e_ready = sem("hidden_e_summed"), sem("hidden_e_ready")
        msg_summed, msg_ready = sem("msg_summed"), sem("msg_ready")
        equal_ready, rows_ready, repeats_ready = sem("equal_ready"), sem("rows_ready"), sem("repeats_ready")
        sums_summed, sums_ready = sem("sums_summed"), sem("sums_ready")
        scattered = sem("scattered")
        x_beta_ready, x_norm_ready, x_norm_rest_ready = sem("x_beta_ready"), sem("x_norm_ready"), sem("x_norm_rest_ready")
        x_transposed, x_copied = sem("x_transposed"), sem("x_copied")
        hidden_n_summed, hidden_n_ready = sem("hidden_n_summed"), sem("hidden_n_ready")
        update_summed, y_norm_ready = sem("update_summed"), sem("y_norm_ready")
        scaled_ready, out_ready = sem("scaled_ready"), sem("out_ready")
        stat_ops, rstd_ready = sem("stat_ops"), sem("rstd_ready")

        block = ctx.enter_context(nc.Block())

        def near_flag(eng):
            eng.wait_ge(near_known, 1)
            return eng.value_load(near[0:1, 0:1], min_val=0, max_val=1)

        N_FOLD, N_WEIGHTS, N_LATE = 4, 8, 4

        @block.sync
        def _(sp):
            sp.dma_start(dst_all[:, :], dst_place.rearrange("(p j) -> p j", p=P)).then_inc(consts_loaded, 16)
            sp.dma_start(const[:, :], consts).then_inc(consts_loaded, 16)

            def transfer(dst, source, done):
                each = N_TILES // PIECES
                for piece in range(PIECES):
                    part = slice(piece * each, (piece + 1) * each)
                    sp.dma_start(dst[:, part, :], source[:, part, :]).then_inc(done, 16)

            def load_edges(s):
                b = s.slot
                wait_apart(sp, gathered[b], s.fills4 * 32 * E_TILES, sp_passed)
                wait_apart(sp, rows_ready, s.n - RING + 1, sp_passed)
                wait_apart(sp, ends_transposed, s.n - RING + 1, sp_passed)
                sp.dma_start(end_idx[b][:, :, :].rearrange("p t c -> p (t c)"), ends_v[s.n]).then_inc(edge_loaded[b], 16)
                sp.dma_start(dst_row[b][:, :], dst_v[bass.ds(s.n, 1), :].broadcast_to([P, E_STEP])).then_inc(edge_loaded[b], 16)
                sp.dma_start(src_in[b][:, :, 1:1 + EDGE_DIM], attr_v[s.n]).then_inc(edge_loaded[b], 16)

            def load_nodes(k):
                b = k.slot
                wait_apart(sp, x_norm_ready, k.n - RING + 1, sp_passed)
                wait_apart(sp, x_norm_rest_ready, k.n - RING + 1, sp_passed)
                wait_apart(sp, x_beta_ready, k.n - RING + 1, sp_passed)
                transfer(x_in[b], rows_v[k.n], x_loaded[b])

            def clear(block):
                wait_apart(sp, cleared[block.slot], 16 * PIECES * block.fills4, sp_passed)
                transfer(table_v[block.n], zeros, cleared[block.slot])

            def body(it):
                if it.mode == EDGES_ONLY and isinstance(it.n, int) and it.n == 0:
                    with sp.Fori(0, NODE_STEPS // RING) as quarter:
                        for phase in range(RING):
                            clear(Step(RING * quarter + phase, phase, quarter))
                    for n in range(NODE_STEPS // RING * RING, NODE_STEPS):
                        clear(Step(n, n % RING, n // RING))
                if it.mode == WHOLE and (block := it.clearing(0)):
                    clear(block)
                if k := it.node(0):
                    b = k.half
                    reach = k.n + 2 if it.mode == WHOLE else EDGE_STEPS
                    wait_apart(sp, scattered, 16 * E_TILES * (min(reach, EDGE_STEPS) if isinstance(reach, int) else reach), sp_passed)
                    wait_apart(sp, hidden_n_summed, k.n - 1, sp_passed)
                    transfer(agg_in[b], table_v[k.n], agg_loaded[b])
                if k := it.node(-3):
                    b = k.half
                    wait_apart(sp, out_ready, k.n + 1, sp_passed)
                    transfer(out_v[k.n], y_out[b], stored[b])
                if (k := it.node(3)) and not (isinstance(k.n, int) and k.n < X_AHEAD):
                    load_nodes(k)
                if (s := it.edge(2)) and not (isinstance(s.n, int) and s.n < EDGES_AHEAD):
                    load_edges(s)

            for n in range(EDGES_AHEAD):
                load_edges(Step(n, n, 0))
            sp.wait_ge(zeros_made, 1)
            sp.dma_start(table[DUMMY:TABLE_ROWS, :], zeros[:, 0, :]).then_inc(dummies_cleared, 16)
            for n in range(X_AHEAD):
                load_nodes(Step(n, n, 0))

            flag = near_flag(sp)
            with sp.If(flag > 0):
                run_pipeline(sp, WHOLE, body)
            with sp.Else():
                run_pipeline(sp, EDGES_ONLY, body)
                run_pipeline(sp, NODES_ONLY, body)
            for b in range(2):
                sp.wait_ge(stored[b], 16 * PIECES * ((NODE_STEPS + 1 - b) // 2))

        @block.gpsimd
        def _(pool):
            nc.gpsimd.memset(zeros[:, :, :], 0.0).then_inc(zeros_made, 1)
            for dst, source in (
                    (coord[:, :, :], node_vec.rearrange("(s p j) -> p s j", p=P, j=N_TILES)),
                    (w_coord_col[:, :], uW1[2 * H:2 * H + 1, :].rearrange("o n -> n o")),
                    (gamma_b[:, 0, :], gamma.rearrange("(o n) -> o n", o=1).broadcast_to([P, H])),
                    (beta_b[:, 0, :], beta.rearrange("(o n) -> o n", o=1).broadcast_to([P, H]))):
                pool.dma_start(dst, source).then_inc(late_loaded, 16)

            def gather(s, t, side, dst):
                nc.gpsimd.indirect_dma_start(
                    out=dst, out_offset=None, in_=rows,
                    in_offset=bass.IndirectOffsetOnAxis(ap=end_idx[s.slot][:, t, side:side + 1], axis=0),
                ).then_inc(gathered[s.slot], 16)

            def body(it):
                new, old = it.edge(0), it.edge(-SCATTER_LAG)
                if new:
                    wait_apart(pool, edge_loaded[new.slot], (new.fills4 + 1) * 48, pool_passed)
                    wait_apart(pool, ends_norm_ready, new.n - RING + 1, pool_passed)
                    wait_apart(pool, ends_transposed, new.n - RING + 1, pool_passed)
                for t in range(E_TILES):
                    if old:
                        if t == 0:
                            wait_apart(pool, sums_ready, old.n + 1, pool_passed)
                            wait_apart(pool, rows_ready, old.n + 1, pool_passed)
                            if isinstance(old.n, int) and old.n == 0:
                                pool.wait_ge(dummies_cleared, 16)
                            if it.mode == WHOLE:
                                if near_clear := it.clearing(1 - SCATTER_LAG):
                                    wait_apart(pool, cleared[near_clear.slot], 16 * PIECES * (near_clear.fills4 + 1), pool_passed)
                                if isinstance(old.n, int) and old.n == 0:
                                    pool.wait_ge(cleared[0], 16 * PIECES)
                            elif isinstance(old.n, int) and old.n == 0:
                                for b in range(RING):
                                    pool.wait_ge(cleared[b], 16 * PIECES * len(range(b, NODE_STEPS, RING)))
                        wait_apart(pool, scattered, 16 * (E_TILES * old.n + t), pool_passed)
                        nc.gpsimd.indirect_dma_start(
                            out=table, out_offset=bass.IndirectOffsetOnAxis(ap=table_row[old.slot][:, t:t + 1], axis=0),
                            in_=sums[old.slot][:, t, :], in_offset=None, compute_op=ALU.add,
                        ).then_inc(scattered, 16)
                    if new:
                        gather(new, t, 0, src_in[new.slot][:, t, 1 + EDGE_DIM:SRC_ROW])
                        gather(new, t, 1, dst_in[new.slot][:, t, :])

            flag = near_flag(pool)
            with pool.If(flag > 0):
                run_pipeline(pool, WHOLE, body)
            with pool.Else():
                run_pipeline(pool, EDGES_ONLY, body)
            pool.wait_ge(scattered, 16 * E_TILES * EDGE_STEPS)

        @block.tensor
        def _(pe):
            def cols(t):
                return slice(t * P, (t + 1) * P)

            def spread_bias(bank, which):
                nc.tensor.matmul(bank, ones_rows[:, :], bias_rows[:, which:which + 1, :].broadcast_to([96, E_TILES, H]),
                                 start=True, stop=False)

            pe.wait_ge(consts_loaded, 32)
            pe.wait_ge(off_most_ready, 1)
            nc.tensor.transpose(ps_f[0:1, 0:P], off_most[:, :], ident).then_inc(off_row_ready, 1)
            pe.wait_ge(fold_loaded, 16 * N_FOLD)
            nc.tensor.transpose(ps_e[:, 0:P], w_msg[:, :], ident).then_inc(weights_multiplied, 1)
            pe.wait_ge(weights_copied, 1)
            nc.tensor.matmul(ps_hid[:, 0:P], w_msg_t[:, :], w_agg[:, :], start=True, stop=True)
            nc.tensor.matmul(ps_upd[0:1, 0:P], mb2_col[:, :], w_agg[:, :], start=True, stop=True).then_inc(weights_multiplied, 1)
            pe.wait_ge(parts_ready, 1)
            for g in range(PART_GROUPS):
                if g >= 2:
                    pe.wait_ge(parts_copied, g - 1)
                bank = (ps_t[0:N_PARTS, 0:E_STEP] if g % 2 == 0 else ps_t[0:N_PARTS, E_STEP:N_STEP]).bitcast(bf16)
                for j in range(N_TILES):
                    if g == 0:
                        last = nc.tensor.transpose(bank[:, cols(j)], wc_cols[:, j, :, :, :].rearrange("p j a w -> p (j a w)"), ident_b[:, :])
                    elif (k := (g - 1) * N_TILES + j) < NODE_STEPS:
                        last = nc.tensor.transpose(bank[:, cols(j)], coord_part[:, k, :, :, :].rearrange("p j a w -> p (j a w)"), ident_b[:, :])
                last.then_inc(parts_transposed, 1)
            pe.wait_ge(parts_copied, PART_GROUPS)
            pe.wait_ge(weights_loaded, 16 * N_WEIGHTS)
            pe.wait_ge(setup_ready, 1)
            pe.wait_ge(bias_spread, 1)

            def body(it):
                nxt, k, own, e, old = it.node(1), it.node(0), it.edge(-1), it.edge(-2), it.edge(-3)
                if k:
                    pe.wait_ge(x_copied, k.n + 1)
                    wait(pe, hidden_n_ready, k.n)
                    pe.wait_ge(agg_loaded[k.half], 16 * PIECES * (k.fills2 + 1))
                    for j in range(N_TILES):
                        if j % E_TILES == 0:
                            bank = slice(j * P, j * P + E_STEP)
                            nc.tensor.matmul(ps_hid[:, bank], w_node[:, :], h_t[k.half][:, bank], start=True, stop=False)
                        nc.tensor.matmul(ps_hid[:, cols(j)], wc_rows[:, j, :], coord_t[:, k.n, :], start=False, stop=False)
                        last = nc.tensor.matmul(ps_hid[:, cols(j)], agg_in[k.half][:, j, :], ident, is_transpose=True,
                                                start=False, stop=j % E_TILES == E_TILES - 1)
                    last.then_inc(hidden_n_summed, 1)
                if old:
                    pe.wait_ge(msg_ready, old.n + 1)
                    pe.wait_ge(equal_ready, old.n + 1)
                    wait(pe, ends_copied, it.edges_upto(-2))
                    for t in range(E_TILES):
                        last = nc.tensor.matmul(ps_f[:, cols(t)], equal[old.slot][:, t, :], msg[:, cols(t)], start=True, stop=True)
                    last.then_inc(sums_summed, 1)
                if e:
                    pe.wait_ge(ends_copied, e.n + 1)
                    wait(pe, msg_ready, e.n)
                    nc.tensor.matmul(ps_e[:, :], w_src[:, :], ends_t[:, 0:E_STEP], start=True, stop=False)
                    nc.tensor.matmul(ps_e[:, :], w_dst[:, :], ends_t[:, E_STEP:], start=False, stop=False)
                    nc.tensor.matmul(ps_e[:, :], w_feat[:, :], feat_t[:, :], start=False, stop=True).then_inc(hidden_e_summed, 1)
                if nxt:
                    pe.wait_ge(x_norm_ready, nxt.n + 1)
                    pe.wait_ge(x_norm_rest_ready, nxt.n + 1)
                    wait(pe, x_copied, nxt.n)
                    wait(pe, ends_copied, it.edges_upto(-2))
                    for j in range(N_TILES):
                        last = nc.tensor.transpose(ps_t[:, cols(j)], x_norm[nxt.half][:, j, :], ident)
                    last.then_inc(x_transposed, 1)
                if k:
                    pe.wait_ge(hidden_n_ready, k.n + 1)
                    for j in range(N_TILES):
                        if j % E_TILES == 0:
                            wait(pe, y_norm_ready, 2 * k.n - 1 + j // E_TILES)
                            spread_bias(ps_upd[:, j * P:j * P + E_STEP], 1)
                        nc.tensor.matmul(ps_upd[:, cols(j)], hidden_n[:, cols(j)], w_out[:, :], start=False, stop=False)
                        last = nc.tensor.matmul(ps_upd[:, cols(j)], h_t[k.half][:, cols(j)], ident, is_transpose=True,
                                                start=False, stop=j % E_TILES == E_TILES - 1)
                        if j % E_TILES == E_TILES - 1:
                            last.then_inc(update_summed, 1)
                if e:
                    pe.wait_ge(hidden_e_ready, e.n + 1)
                    spread_bias(ps_e[:, :], 0)
                    for t in range(E_TILES):
                        last = nc.tensor.matmul(ps_e[:, cols(t)], hidden_e[:, cols(t)], w_fold[:, :], start=False, stop=t == E_TILES - 1)
                    last.then_inc(msg_summed, 1)
                if own:
                    pe.wait_ge(ends_norm_ready, own.n + 1)
                    wait(pe, ends_copied, own.n)
                    wait(pe, x_copied, it.nodes_upto(1))
                    for t in range(2 * E_TILES):
                        nc.tensor.transpose(ps_t[:, cols(t)], ends_norm[own.half][:, t, :], ident)
                    pe.wait_ge(edge_loaded[own.slot], (own.fills4 + 1) * 48)
                    pe.wait_ge(gathered[own.slot], (own.fills4 + 1) * 32 * E_TILES)
                    pe.wait_ge(feat_joined, own.n + 1)
                    wait(pe, sums_ready, it.edges_upto(-3))
                    for t in range(E_TILES):
                        last = nc.tensor.transpose(ps_f[:, cols(t)], src_in[own.slot][:, t, 0:P], ident)
                    last.then_inc(ends_transposed, 1)

            flag = near_flag(pe)
            with pe.If(flag > 0):
                run_pipeline(pe, WHOLE, body)
            with pe.Else():
                run_pipeline(pe, EDGES_ONLY, body)
                run_pipeline(pe, NODES_ONLY, body)

        @block.scalar
        def _(act):
            for dst, source in (
                    (w_msg[:, :], mW2), (w_agg[:, :], uW1[H:2 * H, :]),
                    (mb2_col[:, :], mb2.rearrange("(p o) -> p o", o=1)),
                    (bias_rest[0:1, 1, 0, :], ub2.rearrange("(o n) -> o n", o=1))):
                act.dma_start(dst, source).then_inc(fold_loaded, 16)
            for dst, source in (
                    (w_src[:, :], mW1[0:H, :]), (w_dst[:, :], mW1[H:2 * H, :]),
                    (w_feat[0:1, :], mW1[2 * H + EDGE_DIM + 1:2 * H + EDGE_DIM + 2, :]),
                    (w_feat[1:1 + EDGE_DIM + 1, :], mW1[2 * H:2 * H + EDGE_DIM + 1, :]),
                    (mb1_col[:, :], mb1.rearrange("(p o) -> p o", o=1)),
                    (w_node[:, :], uW1[0:H, :]), (w_out[:, :], uW2),
                    (ub1_col[:, :], ub1.rearrange("(p o) -> p o", o=1))):
                act.dma_start(dst, source).then_inc(weights_loaded, 16)

            act.wait_ge(weights_multiplied, 1)
            nc.scalar.activation(w_msg_t[:, :], ps_e[:, 0:P], ACT.Copy).then_inc(weights_copied, 1)
            act.wait_ge(weights_multiplied, 2)
            nc.scalar.activation(w_fold[:, :], ps_hid[:, 0:P], ACT.Copy)
            nc.scalar.activation(bias_rest[0:1, 0, 0, :], ps_upd[0:1, 0:P], ACT.Copy).then_inc(weights_copied, 1)
            for g in range(PART_GROUPS):
                act.wait_ge(parts_transposed, g + 1)
                bank = (ps_t[0:N_PARTS, 0:E_STEP] if g % 2 == 0 else ps_t[0:N_PARTS, E_STEP:N_STEP]).bitcast(bf16)
                if g == 0:
                    dst, n = wc_rows[:, :, :], N_TILES
                else:
                    n = min(N_TILES, NODE_STEPS - (g - 1) * N_TILES)
                    dst = coord_t[:, (g - 1) * N_TILES:(g - 1) * N_TILES + n, :]
                nc.scalar.activation(dst.rearrange("q j p -> q (j p)"), bank[:, 0:n * P], ACT.Copy).then_inc(parts_copied, 1)
            act.wait_ge(setup_ready, 1)
            for w in range(3):
                last = nc.scalar.activation(bias_rows[32 * w:32 * w + 1, :, :], bias_part[0:1, :, w, :], ACT.Copy)
            last.then_inc(bias_spread, 1)

            def body(it):
                nxt, near_nxt, k, prev = it.node(2), it.node(1), it.node(0), it.node(-1)
                own, e, old = it.edge(-1), it.edge(-2), it.edge(-3)
                now, was = it.phase, (it.phase - 1) % RING

                def norm(dst, source, c, slot):
                    return nc.scalar.activation(dst, source, ACT.Identity, bias=minus[slot][:, c:c + 1], scale=rstd[slot][:, c:c + 1])

                if own:
                    act.wait_ge(rstd_ready, it.stats_before())
                    act.wait_ge(gathered[own.slot], (own.fills4 + 1) * 32 * E_TILES)
                    wait(act, ends_transposed, own.n - 1)
                    for t in range(E_TILES):
                        norm(ends_norm[own.half][:, E_TILES + t, :], dst_in[own.slot][:, t, 1:], E_TILES + t, was)
                if e:
                    act.wait_ge(ends_transposed, e.n + 1)
                    wait(act, hidden_e_summed, e.n)
                    nc.scalar.activation(ends_t[:, :], ps_t[:, :], ACT.Relu)
                    nc.scalar.activation(feat_t[:, :], ps_f[0:FEAT, :], ACT.Copy).then_inc(ends_copied, 1)
                if old:
                    act.wait_ge(msg_summed, old.n + 1)
                    wait(act, sums_summed, old.n)
                    nc.scalar.activation(msg[:, :], ps_e[:, :], ACT.Copy).then_inc(msg_ready, 1)
                if near_nxt:
                    act.wait_ge(rstd_ready, it.stats_before())
                    act.wait_ge(x_loaded[near_nxt.slot], 16 * PIECES * (near_nxt.fills4 + 1))
                    for j in range(X_EARLY, N_TILES - X_ON_VECTOR):
                        last = norm(x_norm[near_nxt.half][:, j, :], x_in[near_nxt.slot][:, j, 1:], 2 * E_TILES + j, was)
                    last.then_inc(x_norm_ready, 1)
                if k:
                    act.wait_ge(hidden_n_summed, k.n + 1)
                    wait(act, update_summed, 2 * k.n)
                    nc.scalar.activation(hidden_n[:, :], ps_hid[:, :], ACT.Silu, bias=ub1_col[:, :]).then_inc(hidden_n_ready, 1)
                if old:
                    act.wait_ge(sums_summed, old.n + 1)
                    wait(act, scattered, 16 * E_TILES * (old.n - RING + 1))
                    nc.scalar.activation(sums[old.slot][:, :, :].rearrange("p t f -> p (t f)"), ps_f[:, :], ACT.Copy).then_inc(sums_ready, 1)
                if prev:
                    act.wait_ge(rstd_ready, it.stats_before() + 1)
                    act.wait_ge(update_summed, 2 * prev.n + 2)
                    wait(act, scaled_ready, prev.n - 1)
                    for j in range(N_TILES):
                        last = norm(y_norm[prev.half][:, j, :], ps_upd[:, j * P:(j + 1) * P], 2 * E_TILES + N_TILES + j, now)
                        if j % E_TILES == E_TILES - 1:
                            last.then_inc(y_norm_ready, 1)
                if near_nxt:
                    act.wait_ge(x_transposed, near_nxt.n + 1)
                    wait(act, update_summed, 2 * near_nxt.n - 2)
                    nc.scalar.activation(h_t[near_nxt.half][:, :], ps_t[:, :], ACT.Relu).then_inc(x_copied, 1)
                if nxt:
                    act.wait_ge(rstd_ready, it.stats_before() + 1)
                    act.wait_ge(x_loaded[nxt.slot], 16 * PIECES * (nxt.fills4 + 1))
                    wait(act, x_transposed, nxt.n - 1)
                    for j in range(X_EARLY):
                        norm(x_norm[nxt.half][:, j, :], x_in[nxt.slot][:, j, 1:], 2 * E_TILES + j, now)
                if e:
                    act.wait_ge(hidden_e_summed, e.n + 1)
                    wait(act, msg_summed, e.n)
                    nc.scalar.activation(hidden_e[:, :], ps_e[:, :], ACT.Silu, bias=mb1_col[:, :]).then_inc(hidden_e_ready, 1)
                if own:
                    for t in range(E_TILES):
                        last = norm(ends_norm[own.half][:, t, :], src_in[own.slot][:, t, FEAT:], t, was)
                    last.then_inc(ends_norm_ready, 1)

            flag = near_flag(act)
            with act.If(flag > 0):
                run_pipeline(act, WHOLE, body)
            with act.Else():
                run_pipeline(act, EDGES_ONLY, body)
                run_pipeline(act, NODES_ONLY, body)

        STAT_OPS = 13
        HALF = N_TILES // 2
        HALVES = (slice(0, HALF), slice(HALF, N_TILES))

        @block.vector
        def _(dve):
            V = nc.vector

            dve.wait_ge(consts_loaded, 32)
            V.tensor_tensor(off_place[:, :], dst_all[:, :], place, ALU.subtract).then_inc(setup_ops, 1)
            dve.wait_ge(setup_ops, 1)
            V.tensor_tensor(off_square[:, :], off_place[:, :], off_place[:, :], ALU.mult).then_inc(setup_ops, 1)
            dve.wait_ge(setup_ops, 2)
            V.tensor_reduce(off_most[:, :], off_square[:, :], AX.X, ALU.max).then_inc(off_most_ready, 1)
            V.tensor_copy(ident_b[:, :], ident)
            V.memset(bias_rows[:, :, :], 0.0)
            V.memset(ones_rows[:, :], 1.0)
            V.memset(wc_cols[:, :, :, :, :], 0.0).then_inc(setup_ops, 1)
            dve.wait_ge(off_row_ready, 1)
            V.tensor_reduce(off_max[:, :], ps_f[0:1, 0:P], AX.X, ALU.max).then_inc(setup_ops, 1)
            dve.wait_ge(setup_ops, 4)
            V.tensor_scalar(near[:, :], off_max[:, :], float(NEAR) ** 2, None, ALU.is_le).then_inc(near_known, 1)

            dve.wait_ge(late_loaded, 16 * N_LATE)
            done = 4
            for part in range(3):
                c_from, w_from = (coord, w_coord_col[:, :]) if part == 0 else (coord_rest, wc_rest[:, part - 1:part])
                V.tensor_copy(wc_part[:, part:part + 1], w_from)
                V.tensor_copy(coord_part[:, :, :, part, :],
                              c_from[:, :, :].rearrange("p s (j o) -> p (s j) o", o=1).broadcast_to([P, NODE_STEPS * N_TILES, 3])
                              .rearrange("p (s j) w -> p s j w", j=N_TILES)).then_inc(setup_ops, 1)
                done += 1
                dve.wait_ge(setup_ops, done)
                if part < 2:
                    V.tensor_tensor(wc_rest[:, part:part + 1], w_from, wc_part[:, part:part + 1], ALU.subtract)
                    V.tensor_tensor(coord_rest[:, :, :], c_from[:, :, :], coord_part[:, :, :, part, 0], ALU.subtract).then_inc(setup_ops, 1)
                    done += 1
                    dve.wait_ge(setup_ops, done)
            for j in range(N_TILES):
                last = V.tensor_copy(wc_cols[:, j, j, :, :], wc_part[:, :].rearrange("p (o w) -> p o w", o=1).broadcast_to([P, 3, 3]))
            last.then_inc(parts_ready, 1)
            dve.wait_ge(weights_copied, 2)
            for part in range(3):
                V.tensor_copy(bias_part[:, :, part, :], bias_rest[:, :, part, :]).then_inc(setup_ops if part < 2 else setup_ready, 1)
                if part < 2:
                    done += 1
                    dve.wait_ge(setup_ops, done)
                    V.tensor_tensor(bias_rest[:, :, part + 1, :], bias_rest[:, :, part, :], bias_part[:, :, part, :],
                                    ALU.subtract).then_inc(setup_ops, 1)
                    done += 1
                    dve.wait_ge(setup_ops, done)

            def body(it):
                new, nxt, prev = it.edge(0), it.node(2), it.node(-1)
                own, near_nxt, done = it.edge(-1), it.node(1), it.node(-2)
                b, was = it.phase, (it.phase - 1) % RING


                def compare(t):
                    if not own:
                        return
                    if t == 0:
                        dve.wait_ge(edge_loaded[own.slot], (own.fills4 + 1) * 48)
                        wait(dve, sums_summed, own.n - RING + 1)
                    last = V.scalar_tensor_tensor(
                        equal[own.slot][:, t, :], dst_row[own.slot][:, :].rearrange("p (j t) -> p t j", t=E_TILES)[:, t, :],
                        end_idx[own.slot][:, t, 1:2], lower, ALU.is_equal, ALU.mult, accum_out=upto[:, t:t + 1])
                    if t == E_TILES - 1:
                        last.then_inc(equal_ready, 1)

                def mark_repeats():
                    if own:
                        dve.wait_ge(equal_ready, own.n + 1)
                        V.tensor_scalar(repeats[:, :], upto[:, :], -1.0, float(DUMMY + P), ALU.add, ALU.mult).then_inc(repeats_ready, 1)

                def choose_rows():
                    if own:
                        dve.wait_ge(repeats_ready, own.n + 1)
                        wait(dve, scattered, 16 * E_TILES * (own.n - RING + 1))
                        V.scalar_tensor_tensor(table_row[own.slot][:, :], repeats[:, :], dummy_row, end_idx[own.slot][:, :, 1],
                                               ALU.min, ALU.max).then_inc(rows_ready, 1)

                def normalise_x(n):
                    if not near_nxt:
                        return
                    j = N_TILES - X_ON_VECTOR + n
                    c = 2 * E_TILES + j
                    if n == 0:
                        dve.wait_ge(rstd_ready, it.stats_before())
                        wait(dve, x_transposed, near_nxt.n - 1)
                    last = V.tensor_scalar(x_norm[near_nxt.half][:, j, :], x_in[near_nxt.slot][:, j, 1:],
                                           rstd[was][:, c:c + 1], minus[was][:, c:c + 1], ALU.mult, ALU.add)
                    if n == X_ON_VECTOR - 1:
                        last.then_inc(x_norm_rest_ready, 1)

                def scale():
                    if not done:
                        return
                    for part in HALVES:
                        dve.wait_ge(y_norm_ready, 2 * done.n + 2)
                        last = V.tensor_tensor(scaled[:, part, :], y_norm[done.half][:, part, :],
                                               gamma_b[:, :, :].broadcast_to([P, HALF, H]), ALU.mult)
                    last.then_inc(scaled_ready, 1)

                def finish():
                    if not done:
                        return
                    dve.wait_ge(scaled_ready, done.n + 1)
                    dve.wait_ge(x_beta_ready, done.n + 1)
                    wait(dve, stored[done.half], 16 * PIECES * done.fills2)
                    for part in HALVES:
                        last = V.tensor_tensor(y_out[done.half][:, part, :], scaled[:, part, :], x_beta[done.half][:, part, :], ALU.add)
                    last.then_inc(out_ready, 1)

                def add_beta():
                    if not prev:
                        return
                    wait(dve, out_ready, prev.n - 1)
                    for part in HALVES:
                        last = V.tensor_tensor(x_beta[prev.half][:, part, :], x_in[prev.slot][:, part, 1:],
                                               beta_b[:, :, :].broadcast_to([P, HALF, H]), ALU.add)
                    last.then_inc(x_beta_ready, 1)

                if not (new or nxt or prev):
                    scale()
                    finish()
                    for t in range(E_TILES):
                        compare(t)
                    mark_repeats()
                    choose_rows()
                    for n in range(X_ON_VECTOR):
                        normalise_x(n)
                    return

                base = it.stats_before() * STAT_OPS
                lo = 0 if new else 2 * E_TILES if nxt else 2 * E_TILES + N_TILES
                hi = 2 * E_TILES + 2 * N_TILES if prev else 2 * E_TILES + N_TILES if nxt else 2 * E_TILES
                at = slice(lo, hi)
                if nxt:
                    dve.wait_ge(x_loaded[nxt.slot], 16 * PIECES * (nxt.fills4 + 1))
                    for j in range(N_TILES):
                        last = V.bn_stats(stats[:, 2 * E_TILES + j, :], x_in[nxt.slot][:, j, 1:])
                add_beta()
                scale()
                if new:
                    dve.wait_ge(gathered[new.slot], (new.fills4 + 1) * 32 * E_TILES)
                    V.tensor_copy(src_in[new.slot][:, :, 0:1], dst_in[new.slot][:, :, 0:1]).then_inc(feat_joined, 1)
                    for t in range(E_TILES):
                        V.bn_stats(stats[:, t, :], src_in[new.slot][:, t, FEAT:])
                        last = V.bn_stats(stats[:, E_TILES + t, :], dst_in[new.slot][:, t, 1:])
                finish()
                if prev:
                    for j in range(N_TILES):
                        if j % E_TILES == 0:
                            dve.wait_ge(update_summed, 2 * prev.n + 1 + j // E_TILES)
                        last = V.bn_stats(stats[:, 2 * E_TILES + N_TILES + j, :], ps_upd[:, j * P:(j + 1) * P])
                last.then_inc(stat_ops, 1)
                normalise_x(0)
                dve.wait_ge(stat_ops, base + 1)
                V.tensor_tensor(s_sub[:, at], stats[:, at, 1], stats[:, at, 4], ALU.subtract)
                V.tensor_tensor(s_m2[:, at], stats[:, at, 2], stats[:, at, 5], ALU.add)
                V.tensor_tensor(s_add[:, at], stats[:, at, 1], stats[:, at, 4], ALU.add).then_inc(stat_ops, 1)
                normalise_x(1)
                dve.wait_ge(stat_ops, base + 2)
                V.scalar_tensor_tensor(s_sq[:, at], s_sub[:, at], 0.25, s_sub[:, at], ALU.mult, ALU.mult)
                V.tensor_scalar(s_m2s[:, at], s_m2[:, at], 1.0 / H, EPS, ALU.mult, ALU.add).then_inc(stat_ops, 1)
                normalise_x(2)
                dve.wait_ge(stat_ops, base + 3)
                V.tensor_tensor(var[:, at], s_m2s[:, at], s_sq[:, at], ALU.add).then_inc(stat_ops, 1)
                compare(0)
                dve.wait_ge(stat_ops, base + 4)
                V.tensor_scalar(guess[:, at].bitcast(i32), var[:, at].bitcast(i32), -0.5, MAGIC, ALU.mult, ALU.add).then_inc(stat_ops, 1)
                compare(1)
                dve.wait_ge(stat_ops, base + 5)
                V.tensor_tensor(root_a[:, at], guess[:, at], guess[:, at], ALU.mult).then_inc(stat_ops, 1)
                compare(2)
                dve.wait_ge(stat_ops, base + 6)
                V.tensor_tensor(root_b[:, at], root_a[:, at], var[:, at], ALU.mult).then_inc(stat_ops, 1)
                compare(3)
                dve.wait_ge(stat_ops, base + 7)
                V.tensor_scalar(root_c[:, at], root_b[:, at], 0.375, -1.25, ALU.mult, ALU.add).then_inc(stat_ops, 1)
                mark_repeats()
                dve.wait_ge(stat_ops, base + 8)
                V.tensor_tensor(root_d[:, at], root_c[:, at], root_b[:, at], ALU.mult).then_inc(stat_ops, 1)
                dve.wait_ge(stat_ops, base + 9)
                V.scalar_tensor_tensor(halley[:, at], root_d[:, at], 1.875, guess[:, at], ALU.add, ALU.mult).then_inc(stat_ops, 1)
                dve.wait_ge(stat_ops, base + 10)
                V.tensor_tensor(newton_a[:, at], halley[:, at], halley[:, at], ALU.mult).then_inc(stat_ops, 1)
                dve.wait_ge(stat_ops, base + 11)
                V.scalar_tensor_tensor(newton_b[:, at], newton_a[:, at], -0.5, var[:, at], ALU.mult, ALU.mult).then_inc(stat_ops, 1)
                choose_rows()
                dve.wait_ge(stat_ops, base + 12)
                wait(dve, ends_norm_ready, it.edges_upto(-RING))
                wait(dve, x_norm_ready, it.nodes_upto(-2))
                V.scalar_tensor_tensor(rstd[b][:, at], newton_b[:, at], 1.5, halley[:, at], ALU.add, ALU.mult).then_inc(stat_ops, 1)
                dve.wait_ge(stat_ops, base + STAT_OPS)
                V.scalar_tensor_tensor(minus[b][:, at], s_add[:, at], -0.5, rstd[b][:, at], ALU.mult, ALU.mult).then_inc(rstd_ready, 1)

            flag = near_flag(dve)
            with dve.If(flag > 0):
                run_pipeline(dve, WHOLE, body)
            with dve.Else():
                run_pipeline(dve, EDGES_ONLY, body)
                run_pipeline(dve, NODES_ONLY, body)


def kernel(x, src, dst, edge_attr_32, node_vec, L0_gnn_mW1, L0_gnn_mb1, L0_gnn_mW2, L0_gnn_mb2, L0_gnn_uW1,
           L0_gnn_ub1, L0_gnn_uW2, L0_gnn_ub2, L0_gnn_ln_gamma, L0_gnn_ln_beta):
    import numpy as np
    import concourse.bacc as bacc
    from concourse.bass_utils import run_bass_kernel_spmd

    x, node_vec, src, dst, attr = (np.asarray(a) for a in (x, node_vec, src, dst, edge_attr_32))
    vec = np.zeros(NODES_PAD, node_vec.dtype)
    vec[:NODES] = node_vec
    rows = np.zeros((NODES_PAD, ROW), x.dtype)
    rows[:NODES, 1:] = x
    rows[:NODES, 0] = node_vec
    ends = np.full((EDGES_PAD, 2), NODES, src.dtype)
    ends[:EDGES, 0] = src
    ends[:EDGES, 1] = dst
    dst_place = np.full(EDGES_PAD, NODES, dst.dtype)
    dst_place[:EDGES] = dst
    attr_pad = np.zeros((EDGES_PAD, EDGE_DIM), attr.dtype)
    attr_pad[:EDGES] = attr
    consts = np.zeros((P, C_COLS), np.float32)
    consts[:, C_IDENT:C_IDENT + P] = np.eye(P)
    consts[:, C_LOWER:C_LOWER + P] = np.tri(P)
    consts[:, C_DUMMY] = DUMMY + np.arange(P)
    consts[:, C_PLACE:] = (np.arange(EDGES_PAD) * (NODES // EDGES)).reshape(P, EDGE_COLS)

    arrays = {"rows": rows, "ends": ends, "dst": dst_place, "attr": attr_pad, "node_vec": vec,
              "mW1": L0_gnn_mW1, "mb1": L0_gnn_mb1, "mW2": L0_gnn_mW2, "mb2": L0_gnn_mb2,
              "uW1": L0_gnn_uW1, "ub1": L0_gnn_ub1, "uW2": L0_gnn_uW2, "ub2": L0_gnn_ub2,
              "gamma": L0_gnn_ln_gamma, "beta": L0_gnn_ln_beta, "consts": consts}
    nc = bacc.Bacc("TRN2", target_bir_lowering=False, num_devices=1)
    arrays = {f"in_{n}": np.ascontiguousarray(a) for n, a in arrays.items()}
    args = [nc.dram_tensor(n, a.shape, mybir.dt.from_np(a.dtype), kind="ExternalInput").ap() for n, a in arrays.items()]
    out = nc.dram_tensor("out", (NODES_PAD, H), mybir.dt.float32, kind="ExternalOutput").ap()
    gnn_layer(nc, *args, out)
    result = run_bass_kernel_spmd(nc, [arrays], core_ids=[0])
    return result.results[0]["out"][:NODES]
```
